# Optimizing a Trainium2 kernel written in Bass

```python
import numpy as np
import jax
import jax.numpy as jnp

def _softmax(x, axis=-1):
    return jax.nn.softmax(x, axis=axis)

def _gelu(x):
    return jax.nn.gelu(x, approximate=True)

def _silu(x):
    return jax.nn.silu(x)

def _sigmoid(x):
    return jax.nn.sigmoid(x)

def _layernorm(x, axis=-1, eps=1e-05):
    m = jnp.mean(x, axis=axis, keepdims=True)
    v = jnp.var(x, axis=axis, keepdims=True)
    return (x - m) / jnp.sqrt(v + eps)

def _scatter_add(tgt, idx, src, axis=0):
    return tgt.at[idx].add(src)

def _segment_sum(src, seg, n):
    return jax.ops.segment_sum(src, seg, n)
kernel_name = 'mk_dlrm_tower_d1_rec_r8_f7c4b3'

def setup_inputs(seed: int=0):
    np.random.seed(seed)
    _w = jnp.asarray

    def _rec_inputs():
        import jax
        import jax.numpy as jnp
        _tk = jax.random.key(seed)
        ids = jnp.stack([jax.random.randint(jax.random.fold_in(_tk, 200 + f), (2048,), 0, v, jnp.int32) for f, v in enumerate([12500, 1250, 125000, 12500, 1000, 12500, 1000, 12500, 125000, 1000, 1000, 1000, 1000, 125000, 12500, 1250, 1000, 1250, 1250, 12500, 12500, 1000, 12500, 1000, 1250, 1250])], axis=1)
        tbl_0 = 0.05 * jax.random.normal(jax.random.fold_in(_tk, 500 + 0), (12500, 64), jnp.float32)
        tbl_1 = 0.05 * jax.random.normal(jax.random.fold_in(_tk, 500 + 1), (1250, 64), jnp.float32)
        tbl_2 = 0.05 * jax.random.normal(jax.random.fold_in(_tk, 500 + 2), (125000, 64), jnp.float32)
        tbl_3 = 0.05 * jax.random.normal(jax.random.fold_in(_tk, 500 + 3), (12500, 64), jnp.float32)
        tbl_4 = 0.05 * jax.random.normal(jax.random.fold_in(_tk, 500 + 4), (1000, 64), jnp.float32)
        tbl_5 = 0.05 * jax.random.normal(jax.random.fold_in(_tk, 500 + 5), (12500, 64), jnp.float32)
        tbl_6 = 0.05 * jax.random.normal(jax.random.fold_in(_tk, 500 + 6), (1000, 64), jnp.float32)
        tbl_7 = 0.05 * jax.random.normal(jax.random.fold_in(_tk, 500 + 7), (12500, 64), jnp.float32)
        tbl_8 = 0.05 * jax.random.normal(jax.random.fold_in(_tk, 500 + 8), (125000, 64), jnp.float32)
        tbl_9 = 0.05 * jax.random.normal(jax.random.fold_in(_tk, 500 + 9), (1000, 64), jnp.float32)
        tbl_10 = 0.05 * jax.random.normal(jax.random.fold_in(_tk, 500 + 10), (1000, 64), jnp.float32)
        tbl_11 = 0.05 * jax.random.normal(jax.random.fold_in(_tk, 500 + 11), (1000, 64), jnp.float32)
        tbl_12 = 0.05 * jax.random.normal(jax.random.fold_in(_tk, 500 + 12), (1000, 64), jnp.float32)
        tbl_13 = 0.05 * jax.random.normal(jax.random.fold_in(_tk, 500 + 13), (125000, 64), jnp.float32)
        tbl_14 = 0.05 * jax.random.normal(jax.random.fold_in(_tk, 500 + 14), (12500, 64), jnp.float32)
        tbl_15 = 0.05 * jax.random.normal(jax.random.fold_in(_tk, 500 + 15), (1250, 64), jnp.float32)
        tbl_16 = 0.05 * jax.random.normal(jax.random.fold_in(_tk, 500 + 16), (1000, 64), jnp.float32)
        tbl_17 = 0.05 * jax.random.normal(jax.random.fold_in(_tk, 500 + 17), (1250, 64), jnp.float32)
        tbl_18 = 0.05 * jax.random.normal(jax.random.fold_in(_tk, 500 + 18), (1250, 64), jnp.float32)
        tbl_19 = 0.05 * jax.random.normal(jax.random.fold_in(_tk, 500 + 19), (12500, 64), jnp.float32)
        tbl_20 = 0.05 * jax.random.normal(jax.random.fold_in(_tk, 500 + 20), (12500, 64), jnp.float32)
        tbl_21 = 0.05 * jax.random.normal(jax.random.fold_in(_tk, 500 + 21), (1000, 64), jnp.float32)
        tbl_22 = 0.05 * jax.random.normal(jax.random.fold_in(_tk, 500 + 22), (12500, 64), jnp.float32)
        tbl_23 = 0.05 * jax.random.normal(jax.random.fold_in(_tk, 500 + 23), (1000, 64), jnp.float32)
        tbl_24 = 0.05 * jax.random.normal(jax.random.fold_in(_tk, 500 + 24), (1250, 64), jnp.float32)
        tbl_25 = 0.05 * jax.random.normal(jax.random.fold_in(_tk, 500 + 25), (1250, 64), jnp.float32)
        _rk = jax.random.fold_in(_tk, 7)
        r_dense_t = 7.22013e-05 + 1.00017 * jax.random.normal(jax.random.fold_in(_rk, 101), (2048, 256), jnp.float32)
        W_top1 = 0.0360844 * jax.random.normal(jax.random.fold_in(_tk, 801), (768, 512), jnp.float32)
        W_top2 = 0.0441942 * jax.random.normal(jax.random.fold_in(_tk, 802), (512, 256), jnp.float32)
        W_top3 = 0.0625 * jax.random.normal(jax.random.fold_in(_tk, 803), (256, 1), jnp.float32)
        b_top1 = jnp.zeros((512,), jnp.float32)
        b_top2 = jnp.zeros((256,), jnp.float32)
        return (r_dense_t, ids, tbl_0, tbl_1, tbl_2, tbl_3, tbl_4, tbl_5, tbl_6, tbl_7, tbl_8, tbl_9, tbl_10, tbl_11, tbl_12, tbl_13, tbl_14, tbl_15, tbl_16, tbl_17, tbl_18, tbl_19, tbl_20, tbl_21, tbl_22, tbl_23, tbl_24, tbl_25, W_top1, b_top1, W_top2, b_top2, W_top3)
    r_dense_t, ids, tbl_0, tbl_1, tbl_2, tbl_3, tbl_4, tbl_5, tbl_6, tbl_7, tbl_8, tbl_9, tbl_10, tbl_11, tbl_12, tbl_13, tbl_14, tbl_15, tbl_16, tbl_17, tbl_18, tbl_19, tbl_20, tbl_21, tbl_22, tbl_23, tbl_24, tbl_25, W_top1, b_top1, W_top2, b_top2, W_top3 = _rec_inputs()

    def _L0_rec_setup():
        import jax, jax.numpy as jnp
        import numpy as np
        EPS = 1e-05
        NI = 33
        TRIL_I, TRIL_J = np.tril_indices(NI, k=-1)

        def layer_norm(x, g, b):
            m = jnp.mean(x, axis=-1, keepdims=True)
            v = jnp.mean(jnp.square(x - m), axis=-1, keepdims=True)
            return (x - m) * jax.lax.rsqrt(v + EPS) * g + b
        key = jax.random.key(seed)
        ks = jax.random.split(key, 8)
        B, D_DENSE, N_SP, D_SP = (4096, 256, 26, 64)
        E, PROJ, MAXD, NFLAT = (128, 32, 512, 528)
        dense_t = jax.random.normal(ks[0], (B, D_DENSE), dtype=jnp.float32)
        sparse_t = jax.random.normal(ks[1], (B, N_SP, D_SP), dtype=jnp.float32)
        Wd = jax.random.normal(ks[2], (E, D_DENSE), dtype=jnp.float32) / np.sqrt(D_DENSE)
        Ws = jax.random.normal(ks[3], (E, D_SP), dtype=jnp.float32) / np.sqrt(D_SP)
        Wsi = jax.random.normal(ks[4], (PROJ, N_SP), dtype=jnp.float32) / np.sqrt(N_SP)
        Wl = jax.random.normal(ks[5], (MAXD, NFLAT), dtype=jnp.float32) / np.sqrt(NFLAT)
        gd = jnp.ones((E,), jnp.float32)
        bd = jnp.zeros((E,), jnp.float32)
        gs = jnp.ones((E,), jnp.float32)
        bs = jnp.zeros((E,), jnp.float32)
        gsi = jnp.ones((PROJ,), jnp.float32)
        bsi = jnp.zeros((PROJ,), jnp.float32)
        gl = jnp.ones((MAXD,), jnp.float32)
        bl = jnp.zeros((MAXD,), jnp.float32)
        return {'dense_t': dense_t, 'sparse_t': sparse_t, 'Wd': Wd, 'gd': gd, 'bd': bd, 'Ws': Ws, 'gs': gs, 'bs': bs, 'Wsi': Wsi, 'gsi': gsi, 'bsi': bsi, 'Wl': Wl, 'gl': gl, 'bl': bl, 'dims_in_use': 384}
    _L0_rec_all = _L0_rec_setup()
    _L0_rec_in = {k: v for k, v in _L0_rec_all.items() if k in ('Wd', 'gd', 'bd', 'Ws', 'gs', 'bs', 'Wsi', 'gsi', 'bsi', 'Wl', 'gl', 'bl')}
    del _L0_rec_all
    return {'r_dense_t': r_dense_t, 'ids': ids, 'tbl_0': tbl_0, 'tbl_1': tbl_1, 'tbl_2': tbl_2, 'tbl_3': tbl_3, 'tbl_4': tbl_4, 'tbl_5': tbl_5, 'tbl_6': tbl_6, 'tbl_7': tbl_7, 'tbl_8': tbl_8, 'tbl_9': tbl_9, 'tbl_10': tbl_10, 'tbl_11': tbl_11, 'tbl_12': tbl_12, 'tbl_13': tbl_13, 'tbl_14': tbl_14, 'tbl_15': tbl_15, 'tbl_16': tbl_16, 'tbl_17': tbl_17, 'tbl_18': tbl_18, 'tbl_19': tbl_19, 'tbl_20': tbl_20, 'tbl_21': tbl_21, 'tbl_22': tbl_22, 'tbl_23': tbl_23, 'tbl_24': tbl_24, 'tbl_25': tbl_25, 'W_top1': W_top1, 'b_top1': b_top1, 'W_top2': W_top2, 'b_top2': b_top2, 'W_top3': W_top3, 'L0_rec_Wd': _L0_rec_in['Wd'], 'L0_rec_gd': _L0_rec_in['gd'], 'L0_rec_bd': _L0_rec_in['bd'], 'L0_rec_Ws': _L0_rec_in['Ws'], 'L0_rec_gs': _L0_rec_in['gs'], 'L0_rec_bs': _L0_rec_in['bs'], 'L0_rec_Wsi': _L0_rec_in['Wsi'], 'L0_rec_gsi': _L0_rec_in['gsi'], 'L0_rec_bsi': _L0_rec_in['bsi'], 'L0_rec_Wl': _L0_rec_in['Wl'], 'L0_rec_gl': _L0_rec_in['gl'], 'L0_rec_bl': _L0_rec_in['bl']}

def reference(r_dense_t, ids, tbl_0, tbl_1, tbl_2, tbl_3, tbl_4, tbl_5, tbl_6, tbl_7, tbl_8, tbl_9, tbl_10, tbl_11, tbl_12, tbl_13, tbl_14, tbl_15, tbl_16, tbl_17, tbl_18, tbl_19, tbl_20, tbl_21, tbl_22, tbl_23, tbl_24, tbl_25, W_top1, b_top1, W_top2, b_top2, W_top3, L0_rec_Wd, L0_rec_gd, L0_rec_bd, L0_rec_Ws, L0_rec_gs, L0_rec_bs, L0_rec_Wsi, L0_rec_gsi, L0_rec_bsi, L0_rec_Wl, L0_rec_gl, L0_rec_bl):
    import jax
    import jax.numpy as jnp

    def _L0_rec_ref(dense_t, sparse_t, Wd, gd, bd, Ws, gs, bs, Wsi, gsi, bsi, Wl, gl, bl, dims_in_use):
        import jax, jax.numpy as jnp
        import numpy as np
        EPS = 1e-05
        NI = 33
        TRIL_I, TRIL_J = np.tril_indices(NI, k=-1)

        def layer_norm(x, g, b):
            m = jnp.mean(x, axis=-1, keepdims=True)
            v = jnp.mean(jnp.square(x - m), axis=-1, keepdims=True)
            return (x - m) * jax.lax.rsqrt(v + EPS) * g + b
        x = layer_norm(dense_t @ Wd.T, gd, bd)
        y = layer_norm(jnp.einsum('bnd,ed->bne', sparse_t, Ws), gs, bs)
        y = jnp.einsum('bne,pn->bep', y, Wsi)
        y = layer_norm(y, gsi, bsi)
        y = jnp.swapaxes(y, 1, 2)
        T = jnp.concatenate([x[:, None, :], y], axis=1)
        Z = jnp.einsum('bnd,bmd->bnm', T, T)
        Zflat = Z[:, TRIL_I, TRIL_J]
        out = layer_norm(Zflat @ Wl.T, gl, bl)
        maxd = out.shape[-1]
        mask = (jnp.arange(maxd) < dims_in_use).astype(out.dtype)
        return out * mask
    e = jnp.stack([tbl_0[ids[:, 0]], tbl_1[ids[:, 1]], tbl_2[ids[:, 2]], tbl_3[ids[:, 3]], tbl_4[ids[:, 4]], tbl_5[ids[:, 5]], tbl_6[ids[:, 6]], tbl_7[ids[:, 7]], tbl_8[ids[:, 8]], tbl_9[ids[:, 9]], tbl_10[ids[:, 10]], tbl_11[ids[:, 11]], tbl_12[ids[:, 12]], tbl_13[ids[:, 13]], tbl_14[ids[:, 14]], tbl_15[ids[:, 15]], tbl_16[ids[:, 16]], tbl_17[ids[:, 17]], tbl_18[ids[:, 18]], tbl_19[ids[:, 19]], tbl_20[ids[:, 20]], tbl_21[ids[:, 21]], tbl_22[ids[:, 22]], tbl_23[ids[:, 23]], tbl_24[ids[:, 24]], tbl_25[ids[:, 25]]], axis=1)
    z = _L0_rec_ref(r_dense_t, e, L0_rec_Wd, L0_rec_gd, L0_rec_bd, L0_rec_Ws, L0_rec_gs, L0_rec_bs, L0_rec_Wsi, L0_rec_gsi, L0_rec_bsi, L0_rec_Wl, L0_rec_gl, L0_rec_bl, 384)
    z = z.reshape(z.shape[0], -1)
    h = jnp.concatenate([z, r_dense_t], axis=1)
    h = jnp.maximum(h @ W_top1 + b_top1, 0.0)
    h = jnp.maximum(h @ W_top2 + b_top2, 0.0)
    y = h @ W_top3
    return y

_drawn_inputs = setup_inputs


def setup_inputs(seed=0):
    import zlib

    import numpy as np

    out = dict(_drawn_inputs(seed))
    spreads = {'b_top1': (0.0, 0.1),
     'b_top2': (0.0, 0.1),
     'L0_rec_gd': (1.0, 0.6),
     'L0_rec_bd': (0.0, 0.8),
     'L0_rec_gs': (1.0, 0.6),
     'L0_rec_bs': (0.0, 0.1),
     'L0_rec_gsi': (1.0, 0.2),
     'L0_rec_bsi': (0.0, 0.1),
     'L0_rec_gl': (1.0, 0.2),
     'L0_rec_bl': (0.0, 0.1)}
    factors = {}
    for name, (base, spread) in spreads.items():
        noise = np.random.default_rng([zlib.crc32(name.encode()), seed]).standard_normal(out[name].shape)
        drawn = base * np.exp(spread * noise) if base else spread * noise
        out[name] = jnp.asarray(drawn.astype(out[name].dtype))
    for name, factor in factors.items():
        out[name] = (out[name] * factor).astype(out[name].dtype)
    return out
```

```python
from contextlib import ExitStack

import numpy as np

import concourse.bass as bass
from concourse import mybir

F32 = mybir.dt.float32
F32R = mybir.dt.float32r
I32 = mybir.dt.int32
ALU = mybir.AluOpType
ACT = mybir.ActivationFunctionType
AX = mybir.AxisListType

P = 128
B = 2048
NS = 26
D = 64
E = 128
PR = 32
MAXD = 512
KEEP = 384
DD = 256
H1, H2 = 512, 256
EPS = 1e-5

BLK = 64
TILES = BLK * NS // P
NBLK = B // BLK
SUP = 256
NSUP = B // SUP
GRP = 16
ZC = PR + 2
QS = 8
SLOTS = QS + 1
KT1 = (KEEP + DD) // P
ROWS = sum([12500, 1250, 125000, 12500, 1000, 12500, 1000, 12500, 125000, 1000, 1000, 1000, 1000,
            125000, 12500, 1250, 1000, 1250, 1250, 12500, 12500, 1000, 12500, 1000, 1250, 1250])


def first_sample(t):
    return P * t // NS


def mix_pieces(h):
    out = []
    for t in range(GRP * NS * h // P, (GRP * NS * (h + 1) - 1) // P + 1):
        lo = max(GRP * h, first_sample(t))
        hi = min(GRP * (h + 1) - 1, (P * t + P - 1) // NS)
        out.append((t, lo, hi - lo + 1))
    return out


def dlrm(nc, x_in, out):
    with ExitStack() as ctx:
        def sb(name, shape, dt=F32):
            return ctx.enter_context(nc.sbuf_tensor(name, shape, dt))

        def ps(name):
            return ctx.enter_context(nc.psum_tensor(name, [P, 512], F32))

        def sem(name):
            return ctx.enter_context(nc.semaphore(name))

        ids = sb("ids", [P, (NBLK + 1) * TILES], I32)
        row0 = sb("row0", [P, TILES], I32)
        idx = sb("idx", [P, 4, TILES], I32)
        eye = sb("eye", [P, P])
        ones = sb("ones", [P, PR])
        epsc = sb("epsc", [P, 1])
        wt2 = sb("wt2", [P, E])
        gsb = sb("gsb", [P, E])
        wc2 = sb("wc2", [P, P])
        gram_w = sb("gram_w", [P, P])
        proj_f = sb("proj_f", [P, E])
        proj_h = sb("proj_h", [P, 2, E])
        proj_l = sb("proj_l", [P, 2, E])
        mixrows = sb("mixrows", [P, TILES, PR])
        mixmask = sb("mixmask", [P, TILES, 6])
        mix_w = sb("mix_w", [P, TILES, 6, PR])
        cvec = sb("cvec", [P, PR])
        biasc = sb("biasc", [P, PR])
        small = sb("small", [P, 24])
        vecs = sb("vecs", [P, 34])
        gscol, gdcol, bdcol, gpcol, bpcol = (vecs[:, c:c + 1] for c in range(5))
        bscol = vecs[:, 5:6]
        glc, blc = vecs[:, 6:9], vecs[:, 9:12]
        b1c, b2c, w3c = vecs[:, 12:16], vecs[:, 16:18], vecs[:, 18:20]
        gq = sb("gq", [P, QS])
        bq = sb("bq", [P, QS])
        wdt = sb("wdt", [P, 2, E])
        wz_h = sb("wz_h", [P, SLOTS, MAXD])
        wz_l = sb("wz_l", [P, SLOTS, MAXD])
        w1_h = sb("w1_h", [P, KT1, H1])
        w1_l = sb("w1_l", [P, KT1, H1])
        w2_h = sb("w2_h", [P, 4, H2])
        w2_l = sb("w2_l", [P, 4, H2])
        sel = sb("sel", [P, 2, P])
        emb = sb("emb", [P, 4, TILES * D])
        embt = sb("embt", [P, 7 * P])
        prod = sb("prod", [P, TILES * D])
        wsib = prod[:, :].rearrange("p (v n) -> p v n", n=NS)
        var = sb("var", [P, TILES])
        std = sb("std", [P, TILES])
        rstd = sb("rstd", [P, TILES])
        u_h = sb("u_h", [P, 2, 512])
        u_l = sb("u_l", [P, 2, 512])
        tt = sb("tt", [P, 2, BLK, ZC])
        sq = sb("sq", [P, 2 * GRP, PR])
        ssum = sb("ssum", [P, 2, 2 * GRP])
        sstd = sb("sstd", [P, 2, 2 * GRP])
        srs = sb("srs", [P, 2, 2 * GRP])
        zc = sb("zc", [P, 2, ZC, 32])
        zs = sb("zs", [P, 4, SLOTS, 64])
        zt_f = sb("zt_f", [P, 3, SUP])
        h1_f = sb("h1_f", [P, 4, SUP])
        h2 = h1_f[:, 0:2, :]
        wx_f = h1_f[:, 0:2, :].rearrange("p c b -> p (c b)")
        zn = sb("zn", [P, 2, KEEP])
        part = zn[:, :, :].rearrange("p a k -> p (a k)")[:, 0:MAXD]
        hst = sb("hst", [P, 2, 6])
        hmv = sb("hmv", [P, 2, 2])
        hstd = sb("hstd", [P, 2])
        hrs = sb("hrs", [P, 2])
        dtx = sb("dtx", [P, 2, SUP])
        dt_f = sb("dt_f", [P, 2, SUP])
        dt_l = sb("dt_l", [P, 2, SUP])
        dt_h = sb("dt_h", [P, 2, SUP])
        xb = sb("xb", [P, 2, E])
        xs = sb("xs", [P, SUP])
        xst = sb("xst", [P, 2, 6])
        xmv = sb("xmv", [P, 2, 2])
        xstd = sb("xstd", [P, 2])
        xrs = sb("xrs", [P, 2])
        yrow = sb("yrow", [1, SUP])
        with ExitStack() as staging:
            wz_f = staging.enter_context(nc.sbuf_tensor("wz_f", [P, SLOTS, MAXD], F32))
            w1_f = staging.enter_context(nc.sbuf_tensor("w1_f", [P, KT1, H1], F32))
            w2_f = staging.enter_context(nc.sbuf_tensor("w2_f", [P, 4, H2], F32))
        z_h = sb("z_h", [P, SLOTS, 4, 64])
        z_l = sb("z_l", [P, SLOTS, 4, 64])
        zt_h, zt_l = sb("zt_h", [P, 3, SUP]), sb("zt_l", [P, 3, SUP])
        h1_h, h1_l = sb("h1_h", [P, 4, SUP]), sb("h1_l", [P, 4, SUP])

        bank_t, bank_g, bank_u = ps("bank_t"), ps("bank_g"), ps("bank_u")
        bank_y = [ps("bank_y0"), ps("bank_y1")]
        bank_z = ps("bank_z")
        bank_h = [ps("bank_h0"), ps("bank_h1")]

        def r(ap):
            return ap.bitcast(F32R)

        ld_ids, ld_small, ld_mix, ld_late = sem("ld_ids"), sem("ld_small"), sem("ld_mix"), sem("ld_late")
        ids_ok, idx_ok = sem("ids_ok"), sem("idx_ok")
        rows_in = [sem(f"rows_in{k}") for k in range(4)]
        pre_v, pre_p, pre_a = sem("pre_v"), sem("pre_p"), sem("pre_a")
        late_v, late_a, late_p, part_ok = sem("late_v"), sem("late_a"), sem("late_p"), sem("part_ok")
        ones_ok = sem("ones_ok")
        turned, embt_ok, grammed, prod_ok = sem("turned"), sem("embt_ok"), sem("grammed"), sem("prod_ok")
        var_ok, vclip_ok, std_ok, rstd_ok, scaled = (
            sem("var_ok"), sem("vclip_ok"), sem("std_ok"), sem("rstd_ok"), sem("scaled"))
        mixed, uh_ok, ul_ok, projected = sem("mixed"), sem("uh_ok"), sem("ul_ok"), sem("projected")
        y_ok, sq_ok, ssum_ok, sstd_ok, srs_ok, t_ok = (
            sem("y_ok"), sem("sq_ok"), sem("ssum_ok"), sem("sstd_ok"), sem("srs_ok"), sem("t_ok"))
        xcol_ok, z_done, zc_ok = sem("xcol_ok"), sem("z_done"), sem("zc_ok")
        zs_in = [sem("zs_in0"), sem("zs_in1")]
        zh_ok, zl_ok, sx_ok = sem("zh_ok"), sem("zl_ok"), sem("sx_ok")
        flat_done, hst_ok, hmv_ok, hstd_ok, hrs_ok, zn_ok = (
            sem("flat_done"), sem("hst_ok"), sem("hmv_ok"), sem("hstd_ok"), sem("hrs_ok"), sem("zn_ok"))
        znt_done, zt_ok, zth_ok, ztl_ok = sem("znt_done"), sem("zt_ok"), sem("zth_ok"), sem("ztl_ok")
        dt_in, dth_ok, dtl_ok = sem("dt_in"), sem("dth_ok"), sem("dtl_ok")
        top1_done, h1_ok, h1h_ok, h1l_ok = sem("top1_done"), sem("h1_ok"), sem("h1h_ok"), sem("h1l_ok")
        top2_done, h2_ok, top3_done, y_out = sem("top2_done"), sem("h2_ok"), sem("top3_done"), sem("y_out")
        dtx_in, x_done, xb_ok, xst_ok, xmv_ok, xstd_ok, xrs_ok, xn_ok, xt_done, xs_ok, sx_done = (
            sem("dtx_in"), sem("x_done"), sem("xb_ok"), sem("xst_ok"), sem("xmv_ok"), sem("xstd_ok"),
            sem("xrs_ok"), sem("xn_ok"), sem("xt_done"), sem("xs_ok"), sem("sx_done"))
        stored = sem("stored")

        N_SMALL = 9

        def after(eng, s, value):
            if not isinstance(value, int) or value > 0:
                eng.wait_ge(s, value)

        def over_supers(eng, body):
            for i in (0, 1):
                body(i, lambda n: 0 <= n < NBLK, lambda m: 0 <= m < NSUP)
            with eng.Fori(2, NSUP) as i:
                body(i, lambda n: True, lambda m: True)
            for i in (NSUP, NSUP + 1):
                body(i, lambda n: 0 <= n < NBLK, lambda m: 0 <= m < NSUP)


        block = ctx.enter_context(nc.Block())

        @block.gpsimd
        def _(pool):
            def copy_indices(n, k):
                pool.tensor_copy(idx[:, k, :], ids[:, bass.ds(TILES * n, TILES)]).then_inc(idx_ok, 1)

            def body(i, blocks, supers):
                for k in range(4):
                    n = 4 * i + k
                    if not blocks(n):
                        continue
                    after(pool, mixed, 2 * n - 6)
                    after(pool, rows_in[(k + 1) % 4], 16 * TILES * (i if k < 3 else i + 1)
                          if blocks(n - 3) else 0)
                    pool.wait_ge(idx_ok, n + 1)
                    if blocks(n + 1):
                        copy_indices(n + 1, (k + 1) % 4)
                    for t in range(TILES):
                        pool.indirect_dma_start(
                            emb[:, k, D * t:D * t + D], None, x_in["tables"],
                            bass.IndirectOffsetOnAxis(ap=idx[:, k, t:t + 1], axis=0),
                        ).then_inc(rows_in[k], 16)

            pool.memset(ids[:, NBLK * TILES:], 0).then_inc(ids_ok, 1)
            pool.wait_ge(ids_ok, 2)
            copy_indices(0, 0)
            over_supers(pool, body)

        @block.sync
        def _(sp):
            sp.dma_start(ids[:, 0:NBLK * TILES], x_in["ids"]).then_inc(ld_ids, 16)
            sp.dma_start(row0[:, :], x_in["row0"]).then_inc(ld_ids, 16)
            sp.dma_start(eye[:, :], x_in["eye"]).then_inc(ld_small, 16)
            sp.dma_start(wt2[0:D, :], x_in["wst"]).then_inc(ld_small, 16)
            sp.dma_start(wt2[D:P, :], x_in["wst"]).then_inc(ld_small, 16)
            sp.dma_start(gsb[:, :], x_in["gs"].partition_broadcast(P)).then_inc(ld_small, 16)
            sp.dma_start(vecs[:, 0:20], x_in["vecs"]).then_inc(ld_small, 16)
            sp.dma_start(wdt[:, :, :], x_in["wdt"]).then_inc(ld_small, 16)
            sp.dma_start(mixrows[:, :, :], x_in["mixrows"]).then_inc(ld_small, 16)
            sp.dma_start(mixmask[:, :, :], x_in["mixmask"]).then_inc(ld_small, 16)
            sp.dma_start(wsib, x_in["wsi"].partition_broadcast(P)).then_inc(ld_small, 16)
            sp.dma_start(wz_f[:, 0:QS, :], x_in["wsym"]).then_inc(ld_late, 16)
            sp.dma_start(wx_f, x_in["wx"]).then_inc(ld_late, 16)
            sp.dma_start(gq[:, :], x_in["gq"]).then_inc(ld_late, 16)
            sp.dma_start(bq[:, :], x_in["bq"]).then_inc(ld_late, 16)
            sp.dma_start(sel[:, :, :], x_in["sel"]).then_inc(ld_late, 16)
            sp.dma_start(w1_f[:, :, :], x_in["w1"]).then_inc(ld_late, 16)
            sp.dma_start(w2_f[:, :, :], x_in["w2"]).then_inc(ld_late, 16)

            def move_products(m, half):
                sp.wait_ge(zc_ok, 8 * m + 4 * half + 4)
                after(sp, zl_ok, m)
                for j in range(4):
                    src = zc[PR * j:PR * j + PR, half]
                    to = slice(32 * half, 32 * half + 32)
                    for q in range(4):
                        sp.dma_start(zs[PR * q:PR * q + PR, j, 0:QS, to],
                                     src[:, QS * q:QS * q + QS, :]).then_inc(zs_in[half], 16)
                    for q in range(2):
                        sp.dma_start(zs[PR * q:PR * q + PR, j, QS, to],
                                     src[:, PR + q, :]).then_inc(zs_in[half], 16)

            def body(i, blocks, supers):
                if supers(i):
                    after(sp, x_done, i)
                    sp.dma_start(dtx[:, :, :], x_in["dense_pos"][:, :, bass.ds(SUP * i, SUP)]
                                 ).then_inc(dtx_in, 16)
                if supers(i - 1):
                    move_products(i - 1, 0)
                if supers(i - 2):
                    after(sp, dtl_ok, i - 2)
                    sp.dma_start(dt_f[:, :, :], x_in["dense"][:, :, bass.ds(SUP * i - 2 * SUP, SUP)]
                                 ).then_inc(dt_in, 16)
                if supers(i - 1):
                    move_products(i - 1, 1)

            over_supers(sp, body)
            sp.wait_ge(stored, 16 * NSUP)

        @block.tensor
        def _(pe):
            pe.wait_ge(pre_v, 3)
            pe.transpose(bank_t[:, 0:P], wt2[:, :], eye[:, :]).then_inc(pre_p, 1)
            pe.wait_ge(pre_a, 1)
            pe.matmul(bank_g[:, 0:D], wc2[:, :], wc2[:, 0:D], start=True, stop=True).then_inc(pre_p, 1)
            pe.wait_ge(pre_a, 3)
            pe.wait_ge(pre_v, 11)

            def turn(i, n, k, q):
                pe.wait_ge(rows_in[k], 16 * TILES * (i + 1))
                after(pe, embt_ok, 2 * n + q)
                for c in range(4 * q, 4 + 3 * q):
                    t0 = min(2 * c, TILES - 2)
                    mm = pe.transpose(bank_t[:, P * (c - 4 * q):P * (c - 4 * q) + P],
                                      emb[:, k, D * t0:D * t0 + P], eye[:, :])
                mm.then_inc(turned, 1)

            def gram(n, q):
                pe.wait_ge(embt_ok, 2 * n + q + 1)
                after(pe, prod_ok, 2 * n + q)
                for c in range(4 * q, 4 + 3 * q):
                    whole = c < 6
                    o = P * (c - 4 * q)
                    mm = pe.matmul(bank_g[:, o:o + (P if whole else D)], embt[:, P * c:P * c + P],
                                   gram_w[:, 0 if whole else D:P], start=True, stop=True)
                mm.then_inc(grammed, 1)

            def mix(n, k, q):
                pe.wait_ge(scaled, n + 1)
                after(pe, ul_ok, 2 * n + q)
                for a in range(2):
                    h = 2 * q + a
                    pieces = mix_pieces(h)
                    for c, (t, lo, cnt) in enumerate(pieces):
                        o = PR * (lo - GRP * h)
                        w0 = PR * (lo - first_sample(t))
                        mm = pe.matmul(
                            bank_u[D * a:D * a + D, o:o + PR * cnt], emb[:, k, D * t:D * t + D],
                            mix_w[:, t, :, :].rearrange("p s v -> p (s v)")[:, w0:w0 + PR * cnt],
                            start=(c == 0), stop=(c == len(pieces) - 1), skip_group_check=True)
                mm.then_inc(mixed, 1)

            def project(n, h):
                q, a = h // 2, h % 2
                pe.wait_ge(ul_ok, 2 * n + q + 1)
                after(pe, y_ok, 4 * n + h - 1)
                y = bank_y[a][:, :]
                pe.matmul(y, r(proj_h[:, a, :]), r(u_h[:, q, :]), start=True, stop=False)
                pe.matmul(y, r(proj_l[:, a, :]), r(u_h[:, q, :]), start=False, stop=False)
                pe.matmul(y, r(proj_h[:, a, :]), r(u_l[:, q, :]), start=False, stop=True
                          ).then_inc(projected, 1)

            def products(n, k, q):
                pe.wait_ge(t_ok, 2 * n + q + 1)
                pe.wait_ge(xcol_ok, n + 1)
                after(pe, zc_ok, 2 * n + q)
                for g in range(8):
                    for j in range(4):
                        b = 32 * q + 4 * g + j
                        mm = pe.matmul(bank_z[PR * j:PR * j + PR, ZC * g:ZC * g + ZC],
                                       tt[:, k, b, 0:PR], tt[:, k, b, :], start=True, stop=True)
                mm.then_inc(z_done, 1)

            def flat(m, a):
                pe.wait_ge(zl_ok, m + 1)
                if a == 0:
                    after(pe, h2_ok, m)
                else:
                    after(pe, y_out, m)
                for s in range(SLOTS):
                    zh, zl = (z[:, s, 2 * a:2 * a + 2, :].rearrange("p j g -> p (j g)") for z in (z_h, z_l))
                    pe.matmul(bank_h[a][:, :], r(zh), r(wz_h[:, s, :]), start=(s == 0), stop=False)
                    pe.matmul(bank_h[a][:, :], r(zh), r(wz_l[:, s, :]), start=False, stop=False)
                    mm = pe.matmul(bank_h[a][:, :], r(zl), r(wz_h[:, s, :]), start=False,
                                   stop=(s == SLOTS - 1))
                mm.then_inc(flat_done, 1)

            def turn_z(m, a):
                pe.wait_ge(zn_ok, 2 * m + a + 1)
                for c in range(3):
                    mm = pe.transpose(bank_h[a][:, P * c:P * c + P], zn[:, a, P * c:P * c + P], eye[:, :])
                mm.then_inc(znt_done, 1)

            def top1(m):
                pe.wait_ge(ztl_ok, m + 1)
                pe.wait_ge(dtl_ok, m + 1)
                for c in range(4):
                    o = bank_h[c // 2][:, SUP * (c % 2):SUP * (c % 2) + SUP]
                    w = slice(P * c, P * c + P)
                    for t in range(KT1):
                        hi = zt_h[:, t, :] if t < 3 else dt_h[:, t - 3, :]
                        lo = zt_l[:, t, :] if t < 3 else dt_l[:, t - 3, :]
                        pe.matmul(o, r(w1_h[:, t, w]), r(hi), start=(t == 0), stop=False)
                        pe.matmul(o, r(w1_l[:, t, w]), r(hi), start=False, stop=False)
                        mm = pe.matmul(o, r(w1_h[:, t, w]), r(lo), start=False, stop=(t == KT1 - 1))
                    if c % 2:
                        mm.then_inc(top1_done, 1)

            def top2(m):
                pe.wait_ge(h1l_ok, m + 1)
                for c in range(2):
                    o = bank_h[0][:, SUP * c:SUP * c + SUP]
                    w = slice(P * c, P * c + P)
                    for t in range(4):
                        pe.matmul(o, r(w2_h[:, t, w]), r(h1_h[:, t, :]), start=(t == 0), stop=False)
                        pe.matmul(o, r(w2_l[:, t, w]), r(h1_h[:, t, :]), start=False, stop=False)
                        mm = pe.matmul(o, r(w2_h[:, t, w]), r(h1_l[:, t, :]), start=False, stop=(t == 3))
                mm.then_inc(top2_done, 1)

            def top3(m):
                pe.wait_ge(h2_ok, m + 1)
                for c in range(2):
                    mm = pe.matmul(bank_h[1][0:1, 0:SUP], w3c[:, c:c + 1], h2[:, c, :],
                                   start=(c == 0), stop=(c == 1))
                mm.then_inc(top3_done, 1)

            def dense_x(m, n):
                pe.wait_ge(dtx_in, 16 * (m + 1))
                pe.wait_ge(embt_ok, 2 * n + 2)
                for a in range(2):
                    for c in range(2):
                        mm = pe.matmul(bank_t[:, E * a:E * a + E], dtx[:, c, P * a:P * a + P],
                                       wdt[:, c, :], start=(c == 0), stop=(c == 1))
                mm.then_inc(x_done, 1)

            def turn_x(m, n):
                pe.wait_ge(xn_ok, 2 * m + 2)
                pe.wait_ge(embt_ok, 2 * n + 2)
                for a in range(2):
                    mm = pe.transpose(bank_t[:, P * a:P * a + P], xb[:, a, :], eye[:, :])
                mm.then_inc(xt_done, 1)

            def sum_x(m, n):
                pe.wait_ge(xs_ok, m + 1)
                pe.wait_ge(embt_ok, 2 * n + 2)
                pe.matmul(bank_t[D:D + PR, 0:SUP], ones[:, :],
                          xs[:, :].rearrange("p (g j) -> p j g", j=4), start=True, stop=True
                          ).then_inc(sx_done, 1)

            def late():
                pe.wait_ge(late_v, 3)
                pe.matmul(bank_h[0][:, :], sel[:, 0, :], part, start=True, stop=False)
                pe.matmul(bank_h[0][:, :], sel[:, 1, :], wx_f, start=False, stop=True).then_inc(late_p, 1)

            def body(i, blocks, supers):
                for k in range(4):
                    n = 4 * i + k
                    if k == 1 and supers(i):
                        pe.wait_ge(xb_ok, i + 1)
                    if k == 2 and supers(i):
                        pe.wait_ge(xs_ok, i + 1)
                    if k == 0 and supers(i - 1):
                        pe.wait_ge(sx_ok, i)
                    if blocks(n):
                        turn(i, n, k, 0)
                    if blocks(n - 2):
                        products(n - 2, k % 2, 0)
                    if blocks(n - 1):
                        mix(n - 1, (k - 1) % 4, 0)
                    if blocks(n):
                        gram(n, 0)
                        turn(i, n, k, 1)
                    if blocks(n - 1):
                        project(n - 1, 0)
                    if k == 0 and supers(i - 2):
                        flat(i - 2, 1)
                    if k == 1 and supers(i - 2):
                        turn_z(i - 2, 1)
                    if k == 2 and supers(i - 2):
                        top2(i - 2)
                    if k == 3 and supers(i - 2):
                        top3(i - 2)
                    if k == 3 and supers(i - 1):
                        if isinstance(i, int) and i == 1:
                            pe.wait_ge(late_v, 7)
                            pe.wait_ge(late_a, 3)
                        flat(i - 1, 0)
                    if blocks(n - 1):
                        project(n - 1, 1)
                        mix(n - 1, (k - 1) % 4, 1)
                    if blocks(n):
                        gram(n, 1)
                    if blocks(n - 2):
                        products(n - 2, k % 2, 1)
                    if blocks(n - 1):
                        project(n - 1, 2)
                    if k == 0 and supers(i):
                        dense_x(i, n)
                    if k == 0 and supers(i - 2):
                        turn_z(i - 2, 0)
                    if k == 1 and supers(i):
                        turn_x(i, n)
                    if k == 1 and supers(i - 2):
                        top1(i - 2)
                    if k == 3 and supers(i):
                        sum_x(i, n)
                    if blocks(n - 1):
                        project(n - 1, 3)
                    if isinstance(i, int) and n == 3:
                        late()

            over_supers(pe, body)

        @block.scalar
        def _(act):
            A = nc.scalar.activation
            act.wait_ge(pre_p, 1)
            act.copy(wc2[:, :], bank_t[:, 0:P]).then_inc(pre_a, 1)
            act.wait_ge(pre_p, 2)
            act.wait_ge(pre_v, 4)
            act.mul(gram_w[0:D, 0:D], bank_g[0:D, 0:D], 1.0 / E).then_inc(pre_a, 1)
            act.mul(gram_w[D:P, D:P], bank_g[D:P, 0:D], 1.0 / E).then_inc(pre_a, 1)

            def rows_out(n, q):
                act.wait_ge(turned, 2 * n + q + 1)
                after(act, grammed, 2 * n + q - 1)
                w = P * (4 - q)
                act.copy(embt[:, 512 * q:512 * q + w], bank_t[:, 0:w]).then_inc(embt_ok, 1)

            def products_out(m, n, k, q):
                act.wait_ge(z_done, 2 * n + q + 1)
                half = k // 2
                after(act, zs_in[half], 24 * 16 * m)
                g0 = 16 * (k % 2) + 8 * q
                act.copy(zc[:, half, :, g0:g0 + 8],
                         bank_z[:, 0:8 * ZC].rearrange("p (g c) -> p c g", c=ZC)).then_inc(zc_ok, 1)

            def mixed_hi(n, q):
                act.wait_ge(mixed, 2 * n + q + 1)
                after(act, projected, 4 * n + 2 * q - 2)
                act.copy(r(u_h[:, q, :]), bank_u[:, :]).then_inc(uh_ok, 1)

            def squares(n, k, q):
                act.wait_ge(y_ok, 4 * n + 2 * q + 2)
                after(act, ssum_ok, 2 * n + q)
                A(sq[:, :, :], tt[:, k, 32 * q:32 * q + 32, 0:PR], ACT.Square).then_inc(sq_ok, 1)

            def root_s(n, q):
                act.wait_ge(ssum_ok, 2 * n + q + 1)
                A(sstd[:, q, :], ssum[:, q, :], ACT.Sqrt, bias=epsc[:, 0:1], scale=1.0 / PR
                  ).then_inc(sstd_ok, 1)

            def xcol(m, n, k, part4):
                act.wait_ge(xs_ok, m + 1)
                after(act, z_done, 2 * n - 2)
                act.copy(tt[:, k, :, PR], xs[:, BLK * part4:BLK * part4 + BLK]).then_inc(xcol_ok, 1)

            def late():
                act.wait_ge(late_v, 4)
                act.copy(r(wz_h[:, :, :]), wz_f[:, :, :]).then_inc(late_a, 1)
                act.wait_ge(ld_late, 16 * 7)
                act.copy(r(w1_h[:, :, :]), w1_f[:, :, :]).then_inc(late_a, 1)
                act.copy(r(w2_h[:, :, :]), w2_f[:, :, :]).then_inc(late_a, 1)

            def body(i, blocks, supers):
                for k in range(4):
                    n = 4 * i + k
                    m2 = i - 1 if k < 2 else i
                    if blocks(n - 2):
                        xcol(m2, n - 2, k % 2, (k - 2) % 4)
                    if blocks(n):
                        rows_out(n, 0)
                    if blocks(n - 2):
                        root_s(n - 2, 1)
                        products_out(m2, n - 2, (k - 2) % 4, 0)
                    if blocks(n - 1):
                        mixed_hi(n - 1, 0)
                    if k == 2 and supers(i - 2):
                        m = i - 2
                        after(act, top2_done, m)
                        after(act, top3_done, m)
                        for c in range(4):
                            if c % 2 == 0:
                                act.wait_ge(top1_done, 2 * m + c // 2 + 1)
                            ins = A(h1_f[:, c, :], bank_h[c // 2][:, SUP * (c % 2):SUP * (c % 2) + SUP],
                                    ACT.Relu, bias=b1c[:, c:c + 1])
                        ins.then_inc(h1_ok, 1)
                        act.wait_ge(h1_ok, m + 1)
                        act.copy(r(h1_h[:, :, :]), h1_f[:, :, :]).then_inc(h1h_ok, 1)
                    if blocks(n):
                        rows_out(n, 1)
                    if k == 1 and supers(i - 2):
                        m = i - 2
                        act.wait_ge(znt_done, 2 * m + 2)
                        for c in range(3):
                            ins = A(zt_f[:, c, P:SUP], bank_h[1][:, P * c:P * c + P], ACT.Identity,
                                    scale=glc[:, c:c + 1], bias=blc[:, c:c + 1])
                        ins.then_inc(zt_ok, 1)
                        act.wait_ge(zt_ok, 2 * m + 2)
                        after(act, top1_done, 2 * m)
                        act.copy(r(zt_h[:, :, :]), zt_f[:, :, :]).then_inc(zth_ok, 1)
                        act.wait_ge(dt_in, 16 * (m + 1))
                        act.copy(r(dt_h[:, :, :]), dt_f[:, :, :]).then_inc(dth_ok, 1)
                    if k == 1 and supers(i):
                        act.wait_ge(xmv_ok, i + 1)
                        A(xstd[:, :], xmv[:, :, 1], ACT.Sqrt, bias=epsc[:, 0:1]).then_inc(xstd_ok, 1)
                    if blocks(n - 1):
                        squares(n - 1, (k - 1) % 2, 0)
                        root_s(n - 1, 0)
                        mixed_hi(n - 1, 1)
                    if blocks(n - 2):
                        products_out(m2, n - 2, (k - 2) % 4, 1)
                    if blocks(n):
                        act.wait_ge(vclip_ok, n + 1)
                        A(std[:, :], var[:, :], ACT.Sqrt).then_inc(std_ok, 1)
                    if (k == 3 and supers(i - 1)) or (k == 0 and supers(i - 2)):
                        m, a = (i - 1, 0) if k == 3 else (i - 2, 1)
                        act.wait_ge(hmv_ok, 2 * m + a + 1)
                        A(hstd[:, a:a + 1], hmv[:, a, 1:2], ACT.Sqrt, bias=epsc[:, 0:1]).then_inc(hstd_ok, 1)
                    if k == 0 and supers(i):
                        act.wait_ge(x_done, i + 1)
                        after(act, xt_done, i)
                        act.copy(xb[:, :, :].rearrange("p a e -> p (a e)"), bank_t[:, 0:2 * E]
                                 ).then_inc(xb_ok, 1)
                    if k == 0 and supers(i - 2):
                        m = i - 2
                        act.wait_ge(znt_done, 2 * m + 1)
                        after(act, ztl_ok, m)
                        for c in range(3):
                            ins = A(zt_f[:, c, 0:P], bank_h[0][:, P * c:P * c + P], ACT.Identity,
                                    scale=glc[:, c:c + 1], bias=blc[:, c:c + 1])
                        ins.then_inc(zt_ok, 1)
                    if k == 1 and supers(i):
                        act.wait_ge(xt_done, i + 1)
                        after(act, sx_done, i)
                        after(act, xcol_ok, 4 * i)
                        A(xs[:, :], bank_t[:, 0:SUP], ACT.Identity, scale=gdcol, bias=bdcol
                          ).then_inc(xs_ok, 1)
                    if k == 2 and supers(i - 2):
                        m = i - 2
                        act.wait_ge(top2_done, m + 1)
                        after(act, top3_done, m)
                        for c in range(2):
                            ins = A(h2[:, c, :], bank_h[0][:, SUP * c:SUP * c + SUP], ACT.Relu,
                                    bias=b2c[:, c:c + 1])
                        ins.then_inc(h2_ok, 1)
                    if k == 2 and supers(i - 1):
                        m = i - 1
                        act.wait_ge(zs_in[0], 24 * 16 * (m + 1))
                        act.wait_ge(zs_in[1], 24 * 16 * (m + 1))
                        act.wait_ge(sx_ok, m + 1)
                        after(act, flat_done, 2 * m)
                        act.copy(r(z_h[:, :, :, :]), zs[:, :, :, :].rearrange("p j s g -> p s j g")).then_inc(zh_ok, 1)
                    if k == 3 and supers(i - 2):
                        m = i - 2
                        act.wait_ge(top3_done, m + 1)
                        after(act, stored, 16 * m)
                        act.copy(yrow[:, :], bank_h[1][0:1, 0:SUP]).then_inc(y_out, 1)
                        act.wait_ge(y_out, m + 1)
                        act.dma_start(out[:, bass.ds(SUP * m, SUP)], yrow[:, :]).then_inc(stored, 16)
                    if k == 3 and supers(i):
                        act.wait_ge(sx_done, i + 1)
                        after(act, zl_ok, i)
                        act.copy(zs[D:D + PR, :, QS, :],
                                 bank_t[D:D + PR, 0:SUP].rearrange("p (j g) -> p j g", j=4)
                                 ).then_inc(sx_ok, 1)
                    if blocks(n - 1):
                        squares(n - 1, (k - 1) % 2, 1)
                    if isinstance(i, int) and n == 3:
                        late()

            act.wait_ge(pre_v, 11)
            over_supers(act, body)

        @block.vector
        def _(dve):
            TT = dve.tensor_tensor
            dve.memset(epsc[:, :], EPS)
            dve.memset(ones[:, :], 1.0)
            dve.memset(gram_w[:, :], 0.0)
            dve.memset(proj_h[:, :, :], 0.0)
            dve.memset(proj_l[:, :, :], 0.0)
            dve.memset(zs[:, :, QS, :], 1.0)
            dve.memset(tt[:, :, :, PR + 1:PR + 2], 1.0).then_inc(ones_ok, 1)
            dve.wait_ge(ld_ids, 32)
            drawn = ids[:, 0:NBLK * TILES].rearrange("p (b t) -> p b t", t=TILES)
            TT(drawn, drawn,
               row0[:, :].unsqueeze(1).broadcast_to([P, NBLK, TILES]), ALU.add).then_inc(ids_ok, 1)
            dve.wait_ge(ld_small, 16 * N_SMALL)
            dve.wait_ge(ones_ok, 1)
            dve.tensor_reduce(small[:, 0:1], wt2[:, :], AX.X, ALU.add).then_inc(pre_v, 1)
            dve.wait_ge(pre_v, 1)
            dve.tensor_scalar(small[:, 1:2], small[:, 0:1], 1.0 / E, None, ALU.mult).then_inc(pre_v, 1)
            dve.wait_ge(pre_v, 2)
            dve.tensor_scalar(wt2[:, :], wt2[:, :], small[:, 1:2], None, ALU.subtract).then_inc(pre_v, 1)
            dve.wait_ge(pre_v, 3)
            TT(proj_f[:, :], wt2[:, :], gsb[:, :], ALU.mult).then_inc(pre_v, 1)
            dve.wait_ge(pre_v, 4)
            for a in range(2):
                s = slice(D * a, D * a + D)
                ins = dve.tensor_copy(r(proj_h[s, a, :]), proj_f[s, :])
            ins.then_inc(pre_v, 1)
            dve.wait_ge(pre_v, 5)
            for a in range(2):
                s = slice(D * a, D * a + D)
                TT(r(proj_l[s, a, :]), proj_f[s, :], proj_h[s, a, :], ALU.subtract)
            dve.tensor_reduce(small[:, 2:2 + TILES], mixrows[:, :, :], AX.X, ALU.add).then_inc(pre_v, 1)
            dve.wait_ge(pre_v, 6)
            dve.scalar_tensor_tensor(out=mixrows[:, :, :],
                                     in0=small[:, 2:2 + TILES].unsqueeze(2).broadcast_to([P, TILES, PR]),
                                     scalar=-1.0 / PR, in1=mixrows[:, :, :], op0=ALU.mult, op1=ALU.add
                                     ).then_inc(pre_v, 1)
            dve.wait_ge(pre_v, 7)
            for s in range(6):
                TT(mix_w[:, :, s, :], mixrows[:, :, :],
                   mixmask[:, :, s:s + 1].broadcast_to([P, TILES, PR]), ALU.mult)
            dve.tensor_reduce(cvec[:, :], wsib, AX.X, ALU.add).then_inc(pre_v, 1)
            dve.wait_ge(pre_v, 8)
            dve.tensor_reduce(small[:, 16:17], cvec[:, :], AX.X, ALU.add).then_inc(pre_v, 1)
            dve.wait_ge(pre_v, 9)
            dve.scalar_tensor_tensor(out=biasc[:, :], in0=small[:, 16:17].broadcast_to([P, PR]),
                                     scalar=-1.0 / PR, in1=cvec[:, :], op0=ALU.mult, op1=ALU.add
                                     ).then_inc(pre_v, 1)
            dve.wait_ge(pre_v, 10)
            dve.tensor_scalar(biasc[:, :], biasc[:, :], bscol, None, ALU.mult).then_inc(pre_v, 1)
            dve.wait_ge(pre_v, 11)

            def late():
                dve.wait_ge(ld_late, 16 * 7)
                dve.tensor_scalar(part, wz_f[:, 0, :], bq[:, 0:1], None, ALU.mult).then_inc(part_ok, 1)
                for s in range(1, QS):
                    dve.wait_ge(part_ok, s)
                    dve.scalar_tensor_tensor(out=part, in0=wz_f[:, s, :], scalar=bq[:, s:s + 1], in1=part,
                                             op0=ALU.mult, op1=ALU.add).then_inc(part_ok, 1)
                dve.wait_ge(part_ok, QS)
                dve.tensor_scalar(small[:, 17:18], gpcol, 0.5, None, ALU.mult)
                dve.tensor_scalar(small[:, 18:19], bpcol, E / 2.0, None, ALU.mult).then_inc(late_v, 1)
                dve.tensor_scalar(sel[:, :, :], sel[:, :, :], gpcol, None, ALU.mult).then_inc(late_v, 1)
                dve.wait_ge(late_v, 2)
                dve.tensor_copy(sel[:, 0, 96:97], small[:, 18:19])
                dve.tensor_copy(sel[0:PR, 1, D:D + 1], bpcol[0:PR, :]).then_inc(late_v, 1)
                for s in range(QS):
                    dve.tensor_scalar(wz_f[:, s, :], wz_f[:, s, :], gq[:, s:s + 1], small[:, 17:18],
                                      ALU.mult, ALU.mult)
                dve.wait_ge(late_p, 1)
                dve.tensor_copy(wz_f[:, QS, :], bank_h[0][:, :]).then_inc(late_v, 1)
                dve.wait_ge(late_a, 1)
                TT(r(wz_l[:, :, :]), wz_f[:, :, :], wz_h[:, :, :], ALU.subtract).then_inc(late_v, 1)
                dve.wait_ge(late_a, 3)
                TT(r(w1_l[:, :, :]), w1_f[:, :, :], w1_h[:, :, :],
                   ALU.subtract).then_inc(late_v, 1)
                TT(r(w2_l[:, :, :]), w2_f[:, :, :], w2_h[:, :, :],
                   ALU.subtract).then_inc(late_v, 1)

            def sum_s(n, q):
                dve.wait_ge(sq_ok, 2 * n + q + 1)
                dve.tensor_reduce(ssum[:, q, :], sq[:, :, :], AX.X, ALU.add).then_inc(ssum_ok, 1)

            def scale_t(n, k, q):
                dve.wait_ge(sstd_ok, 2 * n + q + 1)
                dve.reciprocal(srs[:, q, :], sstd[:, q, :]).then_inc(srs_ok, 1)
                dve.wait_ge(srs_ok, 2 * n + q + 1)
                y = tt[:, k, 32 * q:32 * q + 32, 0:PR]
                TT(y, y, srs[:, q, :].unsqueeze(2).broadcast_to([P, 2 * GRP, PR]), ALU.mult
                   ).then_inc(t_ok, 1)

            def mixed_lo(n, q):
                dve.wait_ge(uh_ok, 2 * n + q + 1)
                TT(r(u_l[:, q, :]), bank_u[:, :], u_h[:, q, :], ALU.subtract).then_inc(ul_ok, 1)

            def add_bias(n, k, h):
                dve.wait_ge(projected, 4 * n + h + 1)
                after(dve, z_done, 2 * n - 2)
                TT(tt[:, k, GRP * h:GRP * h + GRP, 0:PR],
                   bank_y[h % 2][:, :].rearrange("p (b v) -> p b v", v=PR),
                   biasc[:, :].unsqueeze(1).broadcast_to([P, GRP, PR]), ALU.add).then_inc(y_ok, 1)

            def times_e(n, k, q):
                dve.wait_ge(grammed, 2 * n + q + 1)
                a, b = 512 * q, min(512 * (q + 1), TILES * D)
                TT(prod[:, a:b], bank_g[:, 0:b - a], emb[:, k, a:b], ALU.mult).then_inc(prod_ok, 1)

            def body(i, blocks, supers):
                for k in range(4):
                    n = 4 * i + k
                    if blocks(n - 2):
                        sum_s(n - 2, 1)
                    if blocks(n - 1):
                        mixed_lo(n - 1, 0)
                    if blocks(n - 2):
                        scale_t(n - 2, k % 2, 1)
                    if blocks(n):
                        times_e(n, k, 0)
                    if k == 2 and supers(i - 2):
                        m = i - 2
                        dve.wait_ge(h1h_ok, m + 1)
                        TT(r(h1_l[:, :, :]), h1_f[:, :, :], h1_h[:, :, :], ALU.subtract).then_inc(h1l_ok, 1)
                    if k == 1 and supers(i):
                        dve.wait_ge(xb_ok, i + 1)
                        for a in range(2):
                            ins = dve.bn_stats(xst[:, a, :], xb[:, a, :])
                        ins.then_inc(xst_ok, 1)
                        dve.wait_ge(ones_ok, 1)
                        dve.wait_ge(xst_ok, i + 1)
                        for a in range(2):
                            ins = dve.bn_aggr(xmv[:, a, :], xst[:, a, :])
                        ins.then_inc(xmv_ok, 1)
                    if blocks(n - 1):
                        add_bias(n - 1, (k - 1) % 2, 0)
                        add_bias(n - 1, (k - 1) % 2, 1)
                        sum_s(n - 1, 0)
                        mixed_lo(n - 1, 1)
                        scale_t(n - 1, (k - 1) % 2, 0)
                    if k == 1 and supers(i - 2):
                        m = i - 2
                        dve.wait_ge(zth_ok, m + 1)
                        TT(r(zt_l[:, :, :]), zt_f[:, :, :], zt_h[:, :, :], ALU.subtract).then_inc(ztl_ok, 1)
                        dve.wait_ge(dth_ok, m + 1)
                        TT(r(dt_l[:, :, :]), dt_f[:, :, :], dt_h[:, :, :], ALU.subtract).then_inc(dtl_ok, 1)
                    if blocks(n):
                        times_e(n, k, 1)
                        dve.wait_ge(prod_ok, 2 * n + 2)
                        dve.tensor_reduce(var[:, :], prod[:, :].rearrange("p (t d) -> p t d", d=D), AX.X,
                                          ALU.add).then_inc(var_ok, 1)
                        dve.wait_ge(var_ok, n + 1)
                        dve.tensor_scalar(var[:, :], var[:, :], 0.0, EPS, ALU.max, ALU.add
                                          ).then_inc(vclip_ok, 1)
                    norm = (k == 3 and supers(i - 1)) or (k == 0 and supers(i - 2))
                    if norm:
                        m, a = (i - 1, 0) if k == 3 else (i - 2, 1)
                        dve.wait_ge(flat_done, 2 * m + a + 1)
                        dve.bn_stats(hst[:, a, :], bank_h[a][:, :]).then_inc(hst_ok, 1)
                        dve.wait_ge(ones_ok, 1)
                        dve.wait_ge(hst_ok, 2 * m + a + 1)
                        dve.bn_aggr(hmv[:, a, :], hst[:, a, :]).then_inc(hmv_ok, 1)
                    if k == 1 and supers(i):
                        dve.wait_ge(xstd_ok, i + 1)
                        dve.reciprocal(xrs[:, :], xstd[:, :]).then_inc(xrs_ok, 1)
                        dve.wait_ge(xrs_ok, i + 1)
                        for a in range(2):
                            dve.tensor_scalar(xb[:, a, :], xb[:, a, :], xmv[:, a, 0:1], xrs[:, a:a + 1],
                                              ALU.subtract, ALU.mult).then_inc(xn_ok, 1)
                    if blocks(n):
                        dve.wait_ge(std_ok, n + 1)
                        dve.reciprocal(rstd[:, :], std[:, :]).then_inc(rstd_ok, 1)
                        dve.wait_ge(rstd_ok, n + 1)
                        e = emb[:, k, :].rearrange("p (t d) -> p t d", d=D)
                        TT(e, e, rstd[:, :].unsqueeze(2).broadcast_to([P, TILES, D]), ALU.mult
                           ).then_inc(scaled, 1)
                    if norm:
                        dve.wait_ge(hstd_ok, 2 * m + a + 1)
                        dve.reciprocal(hrs[:, a:a + 1], hstd[:, a:a + 1]).then_inc(hrs_ok, 1)
                        dve.wait_ge(hrs_ok, 2 * m + a + 1)
                        after(dve, znt_done, 2 * m + a - 1)
                        dve.tensor_scalar(zn[:, a, :], bank_h[a][:, 0:KEEP], hmv[:, a, 0:1],
                                          hrs[:, a:a + 1], ALU.subtract, ALU.mult).then_inc(zn_ok, 1)
                    if k == 2 and supers(i - 1):
                        m = i - 1
                        dve.wait_ge(zh_ok, m + 1)
                        TT(r(z_l[:, :, :, :]), zs[:, :, :, :].rearrange("p j s g -> p s j g"), z_h[:, :, :, :], ALU.subtract).then_inc(zl_ok, 1)
                    if blocks(n - 1):
                        add_bias(n - 1, (k - 1) % 2, 2)
                        add_bias(n - 1, (k - 1) % 2, 3)
                    if isinstance(i, int) and n == 3:
                        late()

            over_supers(dve, body)


def order():
    pos = np.arange(SUP)
    return (SUP * np.arange(NSUP)[:, None] + 64 * (pos % 4) + pos // 4).reshape(-1)


def kernel(**inputs):
    import concourse.bacc as bacc
    from concourse.bass_utils import run_bass_kernel_spmd

    g = {k: np.asarray(v) for k, v in inputs.items()}
    tables = [g[f"tbl_{f}"] for f in range(NS)]
    at = order()
    row = np.arange(BLK * NS).reshape(TILES, P).T
    starts = np.concatenate([[0], np.cumsum([t.shape[0] for t in tables])[:-1]]).astype(np.int32)
    first = np.array([first_sample(t) for t in range(TILES)])
    p, q = np.meshgrid(np.arange(PR), np.arange(PR), indexing="ij")
    hi, lo = np.maximum(p, q) + 1, np.minimum(p, q) + 1
    wl = np.concatenate([g["L0_rec_Wl"], np.zeros((MAXD, 1), np.float32)], axis=1).T
    pair = np.where(p == q, wl.shape[0] - 1, hi * (hi - 1) // 2 + lo)
    wsym = wl[pair].reshape(PR, 4, QS, MAXD).transpose(1, 0, 2, 3).reshape(P, QS, MAXD)
    wx = np.zeros((P, MAXD), np.float32)
    wx[0:PR] = wl[[(v + 1) * v // 2 for v in range(PR)]]
    sel = np.zeros((P, 2, P), np.float32)
    for v in range(PR):
        sel[v::PR, 0, PR + v] = 1.0
        sel[v, 1, v] = 1.0
    dense_t = g["r_dense_t"].T
    w1 = g["W_top1"]
    w1 = np.concatenate([w1[0:KEEP], w1[MAXD:MAXD + DD]], axis=0)

    def tiles_of(w):
        return w.reshape(w.shape[0] // P, P, w.shape[1]).transpose(1, 0, 2)

    def cols(v, n):
        return v.reshape(n, P).T

    def four(v):
        return np.tile(v, 4)[:, None]

    def by_quadrant(v):
        return np.repeat(v.reshape(4, QS), PR, axis=0)

    vecs = [g["L0_rec_gs"][:, None], g["L0_rec_gd"][:, None], g["L0_rec_bd"][:, None],
            four(g["L0_rec_gsi"]), four(g["L0_rec_bsi"]), g["L0_rec_bs"][:, None],
            cols(g["L0_rec_gl"][0:KEEP], 3), cols(g["L0_rec_bl"][0:KEEP], 3),
            cols(g["b_top1"], 4), cols(g["b_top2"], 2), cols(g["W_top3"][:, 0], 2)]
    arrays = {
        "tables": np.concatenate(tables, axis=0),
        "ids": g["ids"][at].reshape(NBLK * TILES, P).T,
        "row0": starts[row % NS],
        "eye": np.eye(P, dtype=np.float32),
        "wst": g["L0_rec_Ws"].T,
        "gs": g["L0_rec_gs"],
        "vecs": np.concatenate(vecs, axis=1),
        "wdt": tiles_of(g["L0_rec_Wd"].T),
        "mixrows": g["L0_rec_Wsi"].T[row % NS],
        "mixmask": (row // NS - first[None, :])[:, :, None] == np.arange(6),
        "wsi": g["L0_rec_Wsi"],
        "wsym": wsym,
        "wx": wx,
        "gq": by_quadrant(g["L0_rec_gsi"]),
        "bq": by_quadrant(g["L0_rec_bsi"]),
        "sel": sel,
        "w1": tiles_of(w1),
        "w2": tiles_of(g["W_top2"]),
        "dense": tiles_of(dense_t),
        "dense_pos": tiles_of(dense_t[:, at]),
    }
    arrays["mixmask"] = arrays["mixmask"].astype(np.float32)
    nc = bacc.Bacc("TRN2", target_bir_lowering=False, num_devices=1)
    aps, feed = {}, {}
    for name, a in arrays.items():
        a = np.ascontiguousarray(a)
        feed[f"in_{name}"] = a
        aps[name] = nc.dram_tensor(f"in_{name}", a.shape, mybir.dt.from_np(a.dtype), kind="ExternalInput").ap()
    out = nc.dram_tensor("out_y", (1, B), F32, kind="ExternalOutput").ap()
    dlrm(nc, aps, out)
    res = run_bass_kernel_spmd(nc, [feed], core_ids=[0])
    return res.results[0]["out_y"].reshape(B, 1)
```

```python
from contextlib import ExitStack

import numpy as np

import concourse.bass as bass
from concourse import mybir

F32 = mybir.dt.float32
F32R = mybir.dt.float32r
I32 = mybir.dt.int32
ALU = mybir.AluOpType
ACT = mybir.ActivationFunctionType
AX = mybir.AxisListType

P = 128
B = 2048
NS = 26
D = 64
E = 128
PR = 32
MAXD = 512
KEEP = 384
DD = 256
H1, H2 = 512, 256
EPS = 1e-5

BLK = 64
TILES = BLK * NS // P
NBLK = B // BLK
SUP = 256
NSUP = B // SUP
GRP = 16
ZC = PR + 2
QS = 8
SLOTS = QS + 1
KT1 = (KEEP + DD) // P
ROWS = sum([12500, 1250, 125000, 12500, 1000, 12500, 1000, 12500, 125000, 1000, 1000, 1000, 1000,
            125000, 12500, 1250, 1000, 1250, 1250, 12500, 12500, 1000, 12500, 1000, 1250, 1250])


def first_sample(t):
    return P * t // NS


def mix_pieces(h):
    out = []
    for t in range(GRP * NS * h // P, (GRP * NS * (h + 1) - 1) // P + 1):
        lo = max(GRP * h, first_sample(t))
        hi = min(GRP * (h + 1) - 1, (P * t + P - 1) // NS)
        out.append((t, lo, hi - lo + 1))
    return out


def dlrm(nc, x_in, out):
    with ExitStack() as ctx:
        def sb(name, shape, dt=F32):
            return ctx.enter_context(nc.sbuf_tensor(name, shape, dt))

        def ps(name):
            return ctx.enter_context(nc.psum_tensor(name, [P, 512], F32))

        def sem(name):
            return ctx.enter_context(nc.semaphore(name))

        ids = sb("ids", [P, (NBLK + 1) * TILES], I32)
        row0 = sb("row0", [P, TILES], I32)
        idx = sb("idx", [P, 4, TILES], I32)
        eye = sb("eye", [P, P])
        ones = sb("ones", [P, PR])
        epsc = sb("epsc", [P, 1])
        wt2 = sb("wt2", [P, E])
        gsb = sb("gsb", [P, E])
        wc2 = sb("wc2", [P, P])
        gram_w = sb("gram_w", [P, P])
        proj_f = sb("proj_f", [P, E])
        proj_h = sb("proj_h", [P, 2, E])
        proj_l = sb("proj_l", [P, 2, E])
        mixrows = sb("mixrows", [P, TILES, PR])
        mixmask = sb("mixmask", [P, TILES, 6])
        mix_w = sb("mix_w", [P, TILES, 6, PR])
        cvec = sb("cvec", [P, PR])
        biasc = sb("biasc", [P, PR])
        small = sb("small", [P, 24])
        vecs = sb("vecs", [P, 34])
        gscol, gdcol, bdcol, gpcol, bpcol = (vecs[:, c:c + 1] for c in range(5))
        bscol = vecs[:, 5:6]
        glc, blc = vecs[:, 6:9], vecs[:, 9:12]
        b1c, b2c, w3c = vecs[:, 12:16], vecs[:, 16:18], vecs[:, 18:20]
        gq = sb("gq", [P, QS])
        bq = sb("bq", [P, QS])
        wdt = sb("wdt", [P, 2, E])
        wz_h = sb("wz_h", [P, SLOTS, MAXD])
        wz_l = sb("wz_l", [P, SLOTS, MAXD])
        w1_h = sb("w1_h", [P, KT1, H1])
        w1_l = sb("w1_l", [P, KT1, H1])
        w2_h = sb("w2_h", [P, 4, H2])
        w2_l = sb("w2_l", [P, 4, H2])
        sel = sb("sel", [P, 2, P])
        emb = sb("emb", [P, 4, TILES * D])
        embt = sb("embt", [P, 7 * P])
        prod = sb("prod", [P, TILES * D])
        wsib = prod[:, :].rearrange("p (v n) -> p v n", n=NS)
        var = sb("var", [P, TILES])
        std = sb("std", [P, TILES])
        rstd = sb("rstd", [P, TILES])
        u_h = sb("u_h", [P, 2, 512])
        u_l = sb("u_l", [P, 2, 512])
        tt = sb("tt", [P, 2, BLK, ZC])
        sq = sb("sq", [P, 2 * GRP, PR])
        ssum = sb("ssum", [P, 2, 2 * GRP])
        sstd = sb("sstd", [P, 2, 2 * GRP])
        srs = sb("srs", [P, 2, 2 * GRP])
        zc = sb("zc", [P, 2, ZC, 32])
        zs = sb("zs", [P, 4, SLOTS, 64])
        zt_f = sb("zt_f", [P, 3, SUP])
        h1_f = sb("h1_f", [P, 4, SUP])
        h2 = h1_f[:, 0:2, :]
        wx_f = h1_f[:, 0:2, :].rearrange("p c b -> p (c b)")
        zn = sb("zn", [P, 2, KEEP])
        part = zn[:, :, :].rearrange("p a k -> p (a k)")[:, 0:MAXD]
        hst = sb("hst", [P, 2, 6])
        hmv = sb("hmv", [P, 2, 2])
        hstd = sb("hstd", [P, 2])
        hrs = sb("hrs", [P, 2])
        dtx = sb("dtx", [P, 2, SUP])
        dt_f = sb("dt_f", [P, 2, SUP])
        dt_l = sb("dt_l", [P, 2, SUP])
        dt_h = sb("dt_h", [P, 2, SUP])
        xb = sb("xb", [P, 2, E])
        xs = sb("xs", [P, SUP])
        xst = sb("xst", [P, 2, 6])
        xmv = sb("xmv", [P, 2, 2])
        xstd = sb("xstd", [P, 2])
        xrs = sb("xrs", [P, 2])
        yrow = sb("yrow", [1, SUP])
        with ExitStack() as staging:
            wz_f = staging.enter_context(nc.sbuf_tensor("wz_f", [P, SLOTS, MAXD], F32))
            w1_f = staging.enter_context(nc.sbuf_tensor("w1_f", [P, KT1, H1], F32))
            w2_f = staging.enter_context(nc.sbuf_tensor("w2_f", [P, 4, H2], F32))
        z_h = sb("z_h", [P, SLOTS, 4, 64])
        z_l = sb("z_l", [P, SLOTS, 4, 64])
        zt_h, zt_l = sb("zt_h", [P, 3, SUP]), sb("zt_l", [P, 3, SUP])
        h1_h, h1_l = sb("h1_h", [P, 4, SUP]), sb("h1_l", [P, 4, SUP])

        bank_t, bank_g, bank_u = ps("bank_t"), ps("bank_g"), ps("bank_u")
        bank_y = [ps("bank_y0"), ps("bank_y1")]
        bank_z = ps("bank_z")
        bank_h = [ps("bank_h0"), ps("bank_h1")]

        def r(ap):
            return ap.bitcast(F32R)

        ld_ids, ld_small, ld_mix, ld_late = sem("ld_ids"), sem("ld_small"), sem("ld_mix"), sem("ld_late")
        ids_ok, idx_ok = sem("ids_ok"), sem("idx_ok")
        rows_in = [sem(f"rows_in{k}") for k in range(4)]
        pre_v, pre_p, pre_a = sem("pre_v"), sem("pre_p"), sem("pre_a")
        late_v, late_a, late_p, part_ok = sem("late_v"), sem("late_a"), sem("late_p"), sem("part_ok")
        ones_ok = sem("ones_ok")
        turned, embt_ok, grammed, prod_ok = sem("turned"), sem("embt_ok"), sem("grammed"), sem("prod_ok")
        var_ok, vclip_ok, std_ok, rstd_ok, scaled = (
            sem("var_ok"), sem("vclip_ok"), sem("std_ok"), sem("rstd_ok"), sem("scaled"))
        mixed, uh_ok, ul_ok, projected = sem("mixed"), sem("uh_ok"), sem("ul_ok"), sem("projected")
        y_ok, sq_ok, ssum_ok, sstd_ok, srs_ok, t_ok = (
            sem("y_ok"), sem("sq_ok"), sem("ssum_ok"), sem("sstd_ok"), sem("srs_ok"), sem("t_ok"))
        xcol_ok, z_done, zc_ok = sem("xcol_ok"), sem("z_done"), sem("zc_ok")
        zs_in = [sem("zs_in0"), sem("zs_in1")]
        zh_ok, sx_ok = sem("zh_ok"), sem("sx_ok")
        zl_ok = [sem("zl_ok0"), sem("zl_ok1")]
        flat_done, hst_ok, hmv_ok, hstd_ok, hrs_ok, zn_ok = (
            sem("flat_done"), sem("hst_ok"), sem("hmv_ok"), sem("hstd_ok"), sem("hrs_ok"), sem("zn_ok"))
        znt_done, zt_ok, zth_ok, ztl_ok = sem("znt_done"), sem("zt_ok"), sem("zth_ok"), sem("ztl_ok")
        dt_in, dth_ok, dtl_ok = sem("dt_in"), sem("dth_ok"), sem("dtl_ok")
        top1_done, h1_ok, h1h_ok, h1l_ok = sem("top1_done"), sem("h1_ok"), sem("h1h_ok"), sem("h1l_ok")
        top2_done, h2_ok, top3_done, y_out = sem("top2_done"), sem("h2_ok"), sem("top3_done"), sem("y_out")
        dtx_in, x_done, xb_ok, xst_ok, xmv_ok, xstd_ok, xrs_ok, xn_ok, xt_done, xs_ok, sx_done = (
            sem("dtx_in"), sem("x_done"), sem("xb_ok"), sem("xst_ok"), sem("xmv_ok"), sem("xstd_ok"),
            sem("xrs_ok"), sem("xn_ok"), sem("xt_done"), sem("xs_ok"), sem("sx_done"))
        stored = sem("stored")

        N_SMALL = 9

        def after(eng, s, value):
            if not isinstance(value, int) or value > 0:
                eng.wait_ge(s, value)

        def over_supers(eng, body):
            for i in (0, 1, 2):
                body(i, lambda n: 0 <= n < NBLK, lambda m: 0 <= m < NSUP)
            with eng.Fori(3, NSUP) as i:
                body(i, lambda n: True, lambda m: True)
            for i in (NSUP, NSUP + 1, NSUP + 2):
                body(i, lambda n: 0 <= n < NBLK, lambda m: 0 <= m < NSUP)


        block = ctx.enter_context(nc.Block())

        @block.gpsimd
        def _(pool):
            def copy_indices(n, k):
                pool.tensor_copy(idx[:, k, :], ids[:, bass.ds(TILES * n, TILES)]).then_inc(idx_ok, 1)

            def body(i, blocks, supers):
                for k in range(4):
                    n = 4 * i + k
                    if not blocks(n):
                        continue
                    after(pool, mixed, 2 * n - 6)
                    after(pool, rows_in[(k + 1) % 4], 16 * TILES * (i if k < 3 else i + 1)
                          if blocks(n - 3) else 0)
                    pool.wait_ge(idx_ok, n + 1)
                    if blocks(n + 1):
                        copy_indices(n + 1, (k + 1) % 4)
                    for t in range(TILES):
                        pool.indirect_dma_start(
                            emb[:, k, D * t:D * t + D], None, x_in["tables"],
                            bass.IndirectOffsetOnAxis(ap=idx[:, k, t:t + 1], axis=0),
                        ).then_inc(rows_in[k], 16)

            pool.memset(ids[:, NBLK * TILES:], 0).then_inc(ids_ok, 1)
            pool.wait_ge(ids_ok, 2)
            copy_indices(0, 0)
            over_supers(pool, body)

        @block.sync
        def _(sp):
            sp.dma_start(ids[:, 0:NBLK * TILES], x_in["ids"]).then_inc(ld_ids, 16)
            sp.dma_start(row0[:, :], x_in["row0"]).then_inc(ld_ids, 16)
            sp.dma_start(eye[:, :], x_in["eye"]).then_inc(ld_small, 16)
            sp.dma_start(wt2[0:D, :], x_in["wst"]).then_inc(ld_small, 16)
            sp.dma_start(wt2[D:P, :], x_in["wst"]).then_inc(ld_small, 16)
            sp.dma_start(gsb[:, :], x_in["gs"].partition_broadcast(P)).then_inc(ld_small, 16)
            sp.dma_start(vecs[:, 0:20], x_in["vecs"]).then_inc(ld_small, 16)
            sp.dma_start(wdt[:, :, :], x_in["wdt"]).then_inc(ld_small, 16)
            sp.dma_start(mixrows[:, :, :], x_in["mixrows"]).then_inc(ld_small, 16)
            sp.dma_start(mixmask[:, :, :], x_in["mixmask"]).then_inc(ld_small, 16)
            sp.dma_start(wsib, x_in["wsi"].partition_broadcast(P)).then_inc(ld_small, 16)
            sp.dma_start(wz_f[:, 0:QS, :], x_in["wsym"]).then_inc(ld_late, 16)
            sp.dma_start(wx_f, x_in["wx"]).then_inc(ld_late, 16)
            sp.dma_start(gq[:, :], x_in["gq"]).then_inc(ld_late, 16)
            sp.dma_start(bq[:, :], x_in["bq"]).then_inc(ld_late, 16)
            sp.dma_start(sel[:, :, :], x_in["sel"]).then_inc(ld_late, 16)
            sp.dma_start(w1_f[:, :, :], x_in["w1"]).then_inc(ld_late, 16)
            sp.dma_start(w2_f[:, :, :], x_in["w2"]).then_inc(ld_late, 16)

            def move_products(m, half):
                sp.wait_ge(zc_ok, 8 * m + 4 * half + 4)
                after(sp, zl_ok[1], m)
                for j in range(4):
                    src = zc[PR * j:PR * j + PR, half]
                    to = slice(32 * half, 32 * half + 32)
                    for q in range(4):
                        sp.dma_start(zs[PR * q:PR * q + PR, j, 0:QS, to],
                                     src[:, QS * q:QS * q + QS, :]).then_inc(zs_in[half], 16)
                    for q in range(2):
                        sp.dma_start(zs[PR * q:PR * q + PR, j, QS, to],
                                     src[:, PR + q, :]).then_inc(zs_in[half], 16)

            def body(i, blocks, supers):
                if supers(i):
                    after(sp, x_done, i)
                    sp.dma_start(dtx[:, :, :], x_in["dense_pos"][:, :, bass.ds(SUP * i, SUP)]
                                 ).then_inc(dtx_in, 16)
                if supers(i - 1):
                    move_products(i - 1, 0)
                if supers(i - 2):
                    after(sp, dtl_ok, i - 2)
                    sp.dma_start(dt_f[:, :, :], x_in["dense"][:, :, bass.ds(SUP * i - 2 * SUP, SUP)]
                                 ).then_inc(dt_in, 16)
                if supers(i - 1):
                    move_products(i - 1, 1)

            over_supers(sp, body)
            sp.wait_ge(stored, 16 * NSUP)

        @block.tensor
        def _(pe):
            pe.wait_ge(pre_v, 3)
            pe.transpose(bank_t[:, 0:P], wt2[:, :], eye[:, :]).then_inc(pre_p, 1)
            pe.wait_ge(pre_a, 1)
            pe.matmul(bank_g[:, 0:D], wc2[:, :], wc2[:, 0:D], start=True, stop=True).then_inc(pre_p, 1)
            pe.wait_ge(pre_a, 3)
            pe.wait_ge(pre_v, 11)

            def turn(i, n, k, q):
                pe.wait_ge(rows_in[k], 16 * TILES * (i + 1))
                after(pe, embt_ok, 2 * n + q)
                for c in range(4 * q, 4 + 3 * q):
                    t0 = min(2 * c, TILES - 2)
                    mm = pe.transpose(bank_t[:, P * (c - 4 * q):P * (c - 4 * q) + P],
                                      emb[:, k, D * t0:D * t0 + P], eye[:, :])
                mm.then_inc(turned, 1)

            def gram(n, q):
                pe.wait_ge(embt_ok, 2 * n + q + 1)
                after(pe, prod_ok, 2 * n + q)
                for c in range(4 * q, 4 + 3 * q):
                    whole = c < 6
                    o = P * (c - 4 * q)
                    mm = pe.matmul(bank_g[:, o:o + (P if whole else D)], embt[:, P * c:P * c + P],
                                   gram_w[:, 0 if whole else D:P], start=True, stop=True)
                mm.then_inc(grammed, 1)

            def mix(n, k, q):
                pe.wait_ge(scaled, n + 1)
                after(pe, ul_ok, 2 * n + q)
                for a in range(2):
                    h = 2 * q + a
                    pieces = mix_pieces(h)
                    for c, (t, lo, cnt) in enumerate(pieces):
                        o = PR * (lo - GRP * h)
                        w0 = PR * (lo - first_sample(t))
                        mm = pe.matmul(
                            bank_u[D * a:D * a + D, o:o + PR * cnt], emb[:, k, D * t:D * t + D],
                            mix_w[:, t, :, :].rearrange("p s v -> p (s v)")[:, w0:w0 + PR * cnt],
                            start=(c == 0), stop=(c == len(pieces) - 1), skip_group_check=True)
                mm.then_inc(mixed, 1)

            def project(n, h):
                q, a = h // 2, h % 2
                pe.wait_ge(ul_ok, 2 * n + q + 1)
                after(pe, y_ok, 4 * n + h - 1)
                y = bank_y[a][:, :]
                pe.matmul(y, r(proj_h[:, a, :]), r(u_h[:, q, :]), start=True, stop=False)
                pe.matmul(y, r(proj_l[:, a, :]), r(u_h[:, q, :]), start=False, stop=False)
                pe.matmul(y, r(proj_h[:, a, :]), r(u_l[:, q, :]), start=False, stop=True
                          ).then_inc(projected, 1)

            def products(n, k, q):
                pe.wait_ge(t_ok, 2 * n + q + 1)
                pe.wait_ge(xcol_ok, n + 1)
                after(pe, zc_ok, 2 * n + q)
                for g in range(8):
                    for j in range(4):
                        b = 32 * q + 4 * g + j
                        mm = pe.matmul(bank_z[PR * j:PR * j + PR, ZC * g:ZC * g + ZC],
                                       tt[:, k, b, 0:PR], tt[:, k, b, :], start=True, stop=True)
                mm.then_inc(z_done, 1)

            def flat(m, a, third):
                if third == 0:
                    pe.wait_ge(zl_ok[a], m + 1)
                    if a == 0:
                        after(pe, h1_ok, 2 * m - 1)
                    else:
                        after(pe, y_out, m)
                for s in range(SLOTS // 3 * third, SLOTS // 3 * (third + 1)):
                    zh, zl = (z[:, s, 2 * a:2 * a + 2, :].rearrange("p j g -> p (j g)") for z in (z_h, z_l))
                    pe.matmul(bank_h[a][:, :], r(zh), r(wz_h[:, s, :]), start=(s == 0), stop=False)
                    pe.matmul(bank_h[a][:, :], r(zh), r(wz_l[:, s, :]), start=False, stop=False)
                    mm = pe.matmul(bank_h[a][:, :], r(zl), r(wz_h[:, s, :]), start=False,
                                   stop=(s == SLOTS - 1))
                if third == 2:
                    mm.then_inc(flat_done, 1)

            def turn_z(m, a):
                pe.wait_ge(zn_ok, 2 * m + a + 1)
                for c in range(3):
                    mm = pe.transpose(bank_h[a][:, P * c:P * c + P], zn[:, a, P * c:P * c + P], eye[:, :])
                mm.then_inc(znt_done, 1)

            def top1(m, pair):
                pe.wait_ge(ztl_ok, m + 1)
                pe.wait_ge(dtl_ok, m + 1)
                for c in (2 * pair, 2 * pair + 1):
                    o = bank_h[pair][:, SUP * (c % 2):SUP * (c % 2) + SUP]
                    w = slice(P * c, P * c + P)
                    for t in range(KT1):
                        hi = zt_h[:, t, :] if t < 3 else dt_h[:, t - 3, :]
                        lo = zt_l[:, t, :] if t < 3 else dt_l[:, t - 3, :]
                        pe.matmul(o, r(w1_h[:, t, w]), r(hi), start=(t == 0), stop=False)
                        pe.matmul(o, r(w1_l[:, t, w]), r(hi), start=False, stop=False)
                        mm = pe.matmul(o, r(w1_h[:, t, w]), r(lo), start=False, stop=(t == KT1 - 1))
                mm.then_inc(top1_done, 1)

            def top2(m):
                pe.wait_ge(h1l_ok, m + 1)
                for c in range(2):
                    o = bank_h[1][:, SUP * c:SUP * c + SUP]
                    w = slice(P * c, P * c + P)
                    for t in range(4):
                        pe.matmul(o, r(w2_h[:, t, w]), r(h1_h[:, t, :]), start=(t == 0), stop=False)
                        pe.matmul(o, r(w2_l[:, t, w]), r(h1_h[:, t, :]), start=False, stop=False)
                        mm = pe.matmul(o, r(w2_h[:, t, w]), r(h1_l[:, t, :]), start=False, stop=(t == 3))
                mm.then_inc(top2_done, 1)

            def top3(m):
                pe.wait_ge(h2_ok, m + 1)
                for c in range(2):
                    mm = pe.matmul(bank_h[1][0:1, 0:SUP], w3c[:, c:c + 1], h2[:, c, :],
                                   start=(c == 0), stop=(c == 1))
                mm.then_inc(top3_done, 1)

            def dense_x(m, n):
                pe.wait_ge(dtx_in, 16 * (m + 1))
                pe.wait_ge(embt_ok, 2 * n + 1)
                for a in range(2):
                    for c in range(2):
                        mm = pe.matmul(bank_t[:, E * a:E * a + E], dtx[:, c, P * a:P * a + P],
                                       wdt[:, c, :], start=(c == 0), stop=(c == 1))
                mm.then_inc(x_done, 1)

            def turn_x(m, n):
                pe.wait_ge(xn_ok, 2 * m + 2)
                pe.wait_ge(embt_ok, 2 * n + 1)
                for a in range(2):
                    mm = pe.transpose(bank_t[:, P * a:P * a + P], xb[:, a, :], eye[:, :])
                mm.then_inc(xt_done, 1)

            def sum_x(m, n, more):
                pe.wait_ge(xs_ok, m + 1)
                if more:
                    pe.wait_ge(embt_ok, 2 * n + 2)
                pe.matmul(bank_t[D:D + PR, 0:SUP], ones[:, :],
                          xs[:, :].rearrange("p (g j) -> p j g", j=4), start=True, stop=True
                          ).then_inc(sx_done, 1)

            def late():
                pe.wait_ge(late_v, 3)
                pe.matmul(bank_h[0][:, :], sel[:, 0, :], part, start=True, stop=False)
                pe.matmul(bank_h[0][:, :], sel[:, 1, :], wx_f, start=False, stop=True).then_inc(late_p, 1)

            def body(i, blocks, supers):
                for k in range(4):
                    n = 4 * i + k
                    if blocks(n - 2):
                        mix(n - 2, (k - 2) % 4, 1)
                    if blocks(n):
                        if k == 1 and supers(i - 1):
                            pe.wait_ge(sx_ok, i)
                        turn(i, n, k, 0)
                    if blocks(n - 2):
                        products(n - 2, k % 2, 0)
                        project(n - 2, 2)
                        project(n - 2, 3)
                    if blocks(n):
                        gram(n, 0)
                    if k == 0 and supers(i):
                        dense_x(i, n)
                    if k == 0 and supers(i - 3):
                        top1(i - 3, 1)
                    if k == 1 and supers(i):
                        turn_x(i, n)
                    if k == 1 and supers(i - 2):
                        flat(i - 2, 0, 2)
                    if k == 1 and supers(i - 3):
                        top2(i - 3)
                    if k == 2 and supers(i - 2):
                        flat(i - 2, 1, 1)
                        flat(i - 2, 1, 2)
                    if blocks(n - 1):
                        mix(n - 1, (k - 1) % 4, 0)
                    if blocks(n):
                        if k == 0 and supers(i):
                            pe.wait_ge(xb_ok, i + 1)
                        if k == 1 and supers(i):
                            pe.wait_ge(xs_ok, i + 1)
                        turn(i, n, k, 1)
                    if blocks(n - 2):
                        products(n - 2, k % 2, 1)
                    if blocks(n - 1):
                        project(n - 1, 0)
                        project(n - 1, 1)
                    if k == 1 and supers(i - 3):
                        top3(i - 3)
                    if blocks(n):
                        gram(n, 1)
                    if k == 0 and supers(i - 1):
                        sum_x(i - 1, n, blocks(n))
                    if k == 0 and supers(i - 2):
                        flat(i - 2, 0, 0)
                        flat(i - 2, 0, 1)
                    if k == 1 and supers(i - 2):
                        turn_z(i - 2, 0)
                        flat(i - 2, 1, 0)
                    if k == 2 and supers(i - 2):
                        turn_z(i - 2, 1)
                    if k == 3 and supers(i - 2):
                        top1(i - 2, 0)
                    if isinstance(i, int) and n == 4:
                        late()
                    if isinstance(i, int) and n == 7:
                        pe.wait_ge(late_v, 7)
                        pe.wait_ge(late_a, 3)

            over_supers(pe, body)

        @block.scalar
        def _(act):
            A = nc.scalar.activation
            act.wait_ge(pre_p, 1)
            act.copy(wc2[:, :], bank_t[:, 0:P]).then_inc(pre_a, 1)
            act.wait_ge(pre_p, 2)
            act.wait_ge(pre_v, 4)
            act.mul(gram_w[0:D, 0:D], bank_g[0:D, 0:D], 1.0 / E).then_inc(pre_a, 1)
            act.mul(gram_w[D:P, D:P], bank_g[D:P, 0:D], 1.0 / E).then_inc(pre_a, 1)

            def rows_out(n, q):
                act.wait_ge(turned, 2 * n + q + 1)
                after(act, grammed, 2 * n + q - 1)
                w = P * (4 - q)
                act.copy(embt[:, 512 * q:512 * q + w], bank_t[:, 0:w]).then_inc(embt_ok, 1)

            def products_out(m, n, k, q):
                act.wait_ge(z_done, 2 * n + q + 1)
                half = k // 2
                after(act, zs_in[half], 24 * 16 * m)
                g0 = 16 * (k % 2) + 8 * q
                act.copy(zc[:, half, :, g0:g0 + 8],
                         bank_z[:, 0:8 * ZC].rearrange("p (g c) -> p c g", c=ZC)).then_inc(zc_ok, 1)

            def mixed_hi(n, q):
                act.wait_ge(mixed, 2 * n + q + 1)
                after(act, projected, 4 * n + 2 * q - 2)
                act.copy(r(u_h[:, q, :]), bank_u[:, :]).then_inc(uh_ok, 1)

            def squares(n, k, q):
                act.wait_ge(y_ok, 4 * n + 2 * q + 2)
                after(act, ssum_ok, 2 * n + q)
                A(sq[:, :, :], tt[:, k, 32 * q:32 * q + 32, 0:PR], ACT.Square).then_inc(sq_ok, 1)

            def root_s(n, q):
                act.wait_ge(ssum_ok, 2 * n + q + 1)
                A(sstd[:, q, :], ssum[:, q, :], ACT.Sqrt, bias=epsc[:, 0:1], scale=1.0 / PR
                  ).then_inc(sstd_ok, 1)

            def xcol(m, n, k, part4):
                act.wait_ge(xs_ok, m + 1)
                after(act, z_done, 2 * n - 2)
                act.copy(tt[:, k, :, PR], xs[:, BLK * part4:BLK * part4 + BLK]).then_inc(xcol_ok, 1)

            def relu1(m, pair):
                act.wait_ge(top1_done, 2 * m + pair + 1)
                if pair == 0:
                    after(act, top3_done, m)
                for c in (2 * pair, 2 * pair + 1):
                    ins = A(h1_f[:, c, :], bank_h[pair][:, SUP * (c % 2):SUP * (c % 2) + SUP],
                            ACT.Relu, bias=b1c[:, c:c + 1])
                ins.then_inc(h1_ok, 1)

            def h1_hi(m):
                after(act, top2_done, m)
                act.wait_ge(h1_ok, 2 * m + 2)
                act.copy(r(h1_h[:, :, :]), h1_f[:, :, :]).then_inc(h1h_ok, 1)

            def relu2(m):
                act.wait_ge(top2_done, m + 1)
                for c in range(2):
                    ins = A(h2[:, c, :], bank_h[1][:, SUP * c:SUP * c + SUP], ACT.Relu,
                            bias=b2c[:, c:c + 1])
                ins.then_inc(h2_ok, 1)

            def store_y(m):
                act.wait_ge(top3_done, m + 1)
                after(act, stored, 16 * m)
                act.copy(yrow[:, :], bank_h[1][0:1, 0:SUP]).then_inc(y_out, 1)
                act.wait_ge(y_out, m + 1)
                act.dma_start(out[:, bass.ds(SUP * m, SUP)], yrow[:, :]).then_inc(stored, 16)

            def root_h(m, a):
                act.wait_ge(hmv_ok, 2 * m + a + 1)
                A(hstd[:, a:a + 1], hmv[:, a, 1:2], ACT.Sqrt, bias=epsc[:, 0:1]).then_inc(hstd_ok, 1)

            def gains_z(m, a):
                act.wait_ge(znt_done, 2 * m + a + 1)
                if a == 0:
                    after(act, ztl_ok, m)
                for c in range(3):
                    ins = A(zt_f[:, c, P * a:P * a + P], bank_h[a][:, P * c:P * c + P], ACT.Identity,
                            scale=glc[:, c:c + 1], bias=blc[:, c:c + 1])
                ins.then_inc(zt_ok, 1)

            def zt_hi(m):
                act.wait_ge(zt_ok, 2 * m + 2)
                after(act, top1_done, 2 * m)
                act.copy(r(zt_h[:, :, :]), zt_f[:, :, :]).then_inc(zth_ok, 1)

            def dt_hi(m):
                act.wait_ge(dt_in, 16 * (m + 1))
                after(act, top1_done, 2 * m)
                act.copy(r(dt_h[:, :, :]), dt_f[:, :, :]).then_inc(dth_ok, 1)

            def z_hi(m, a):
                if a == 0:
                    act.wait_ge(zs_in[0], 24 * 16 * (m + 1))
                    act.wait_ge(zs_in[1], 24 * 16 * (m + 1))
                    act.wait_ge(sx_ok, m + 1)
                    after(act, flat_done, 2 * m)
                act.copy(r(z_h[:, :, 2 * a:2 * a + 2, :]),
                         zs[:, 2 * a:2 * a + 2].rearrange("p j s g -> p s j g")).then_inc(zh_ok, 1)

            def x_out(m):
                act.wait_ge(x_done, m + 1)
                after(act, xt_done, m)
                act.copy(xb[:, :, :].rearrange("p a e -> p (a e)"), bank_t[:, 0:2 * E]).then_inc(xb_ok, 1)

            def root_x(m):
                act.wait_ge(xmv_ok, m + 1)
                A(xstd[:, :], xmv[:, :, 1], ACT.Sqrt, bias=epsc[:, 0:1]).then_inc(xstd_ok, 1)

            def gains_x(m):
                act.wait_ge(xt_done, m + 1)
                after(act, sx_done, m)
                after(act, xcol_ok, 4 * m)
                A(xs[:, :], bank_t[:, 0:SUP], ACT.Identity, scale=gdcol, bias=bdcol).then_inc(xs_ok, 1)

            def sum_x_out(m):
                act.wait_ge(sx_done, m + 1)
                after(act, zl_ok[1], m)
                act.copy(zs[D:D + PR, :, QS, :],
                         bank_t[D:D + PR, 0:SUP].rearrange("p (j g) -> p j g", j=4)).then_inc(sx_ok, 1)

            def root_e(n):
                act.wait_ge(vclip_ok, n + 1)
                A(std[:, :], var[:, :], ACT.Sqrt).then_inc(std_ok, 1)

            def late():
                act.wait_ge(late_v, 4)
                act.copy(r(wz_h[:, :, :]), wz_f[:, :, :]).then_inc(late_a, 1)
                act.wait_ge(ld_late, 16 * 7)
                act.copy(r(w1_h[:, :, :]), w1_f[:, :, :]).then_inc(late_a, 1)
                act.copy(r(w2_h[:, :, :]), w2_f[:, :, :]).then_inc(late_a, 1)

            def body(i, blocks, supers):
                for k in range(4):
                    n = 4 * i + k
                    m2 = i - 1 if k < 2 else i
                    if k == 1 and supers(i - 1):
                        sum_x_out(i - 1)
                    if blocks(n - 2):
                        xcol(m2, n - 2, k % 2, (k - 2) % 4)
                        mixed_hi(n - 2, 1)
                    if blocks(n):
                        rows_out(n, 0)
                    if k == 0 and supers(i - 3):
                        relu1(i - 3, 0)
                    if k == 3 and supers(i - 2):
                        gains_z(i - 2, 1)
                        zt_hi(i - 2)
                    if blocks(n - 2):
                        products_out(m2, n - 2, (k - 2) % 4, 0)
                    if blocks(n - 1):
                        root_e(n - 1)
                    if k == 2 and supers(i - 2):
                        gains_z(i - 2, 0)
                    if blocks(n - 2):
                        squares(n - 2, k % 2, 1)
                    if k == 0 and supers(i):
                        x_out(i)
                    if k == 1 and supers(i):
                        gains_x(i)
                    if k == 2 and supers(i - 2):
                        dt_hi(i - 2)
                    if blocks(n - 2):
                        root_s(n - 2, 1)
                    if k == 3 and supers(i - 1):
                        z_hi(i - 1, 0)
                    if blocks(n - 1):
                        mixed_hi(n - 1, 0)
                    if k == 0 and supers(i - 3):
                        relu1(i - 3, 1)
                    if k == 1 and supers(i - 3):
                        relu2(i - 3)
                    if blocks(n):
                        rows_out(n, 1)
                    if k == 0 and supers(i):
                        root_x(i)
                    if k == 1 and supers(i - 3):
                        store_y(i - 3)
                    if blocks(n - 2):
                        products_out(m2, n - 2, (k - 2) % 4, 1)
                    if k == 0 and supers(i - 3):
                        h1_hi(i - 3)
                    if k == 1 and supers(i - 2):
                        root_h(i - 2, 0)
                    if k == 2 and supers(i - 2):
                        root_h(i - 2, 1)
                    if blocks(n - 1):
                        squares(n - 1, (k - 1) % 2, 0)
                    if k == 3 and supers(i - 1):
                        z_hi(i - 1, 1)
                    if blocks(n - 1):
                        root_s(n - 1, 0)
                    if isinstance(i, int) and n == 5:
                        late()

            act.wait_ge(pre_v, 11)
            over_supers(act, body)

        @block.vector
        def _(dve):
            TT = dve.tensor_tensor
            dve.memset(epsc[:, :], EPS)
            dve.memset(ones[:, :], 1.0)
            dve.memset(gram_w[:, :], 0.0)
            dve.memset(proj_h[:, :, :], 0.0)
            dve.memset(proj_l[:, :, :], 0.0)
            dve.memset(zs[:, :, QS, :], 1.0)
            dve.memset(tt[:, :, :, PR + 1:PR + 2], 1.0).then_inc(ones_ok, 1)
            dve.wait_ge(ld_ids, 32)
            drawn = ids[:, 0:NBLK * TILES].rearrange("p (b t) -> p b t", t=TILES)
            TT(drawn, drawn,
               row0[:, :].unsqueeze(1).broadcast_to([P, NBLK, TILES]), ALU.add).then_inc(ids_ok, 1)
            dve.wait_ge(ld_small, 16 * N_SMALL)
            dve.wait_ge(ones_ok, 1)
            dve.tensor_reduce(small[:, 0:1], wt2[:, :], AX.X, ALU.add).then_inc(pre_v, 1)
            dve.wait_ge(pre_v, 1)
            dve.tensor_scalar(small[:, 1:2], small[:, 0:1], 1.0 / E, None, ALU.mult).then_inc(pre_v, 1)
            dve.wait_ge(pre_v, 2)
            dve.tensor_scalar(wt2[:, :], wt2[:, :], small[:, 1:2], None, ALU.subtract).then_inc(pre_v, 1)
            dve.wait_ge(pre_v, 3)
            TT(proj_f[:, :], wt2[:, :], gsb[:, :], ALU.mult).then_inc(pre_v, 1)
            dve.wait_ge(pre_v, 4)
            for a in range(2):
                s = slice(D * a, D * a + D)
                ins = dve.tensor_copy(r(proj_h[s, a, :]), proj_f[s, :])
            ins.then_inc(pre_v, 1)
            dve.wait_ge(pre_v, 5)
            for a in range(2):
                s = slice(D * a, D * a + D)
                TT(r(proj_l[s, a, :]), proj_f[s, :], proj_h[s, a, :], ALU.subtract)
            dve.tensor_reduce(small[:, 2:2 + TILES], mixrows[:, :, :], AX.X, ALU.add).then_inc(pre_v, 1)
            dve.wait_ge(pre_v, 6)
            dve.scalar_tensor_tensor(out=mixrows[:, :, :],
                                     in0=small[:, 2:2 + TILES].unsqueeze(2).broadcast_to([P, TILES, PR]),
                                     scalar=-1.0 / PR, in1=mixrows[:, :, :], op0=ALU.mult, op1=ALU.add
                                     ).then_inc(pre_v, 1)
            dve.wait_ge(pre_v, 7)
            for s in range(6):
                TT(mix_w[:, :, s, :], mixrows[:, :, :],
                   mixmask[:, :, s:s + 1].broadcast_to([P, TILES, PR]), ALU.mult)
            dve.tensor_reduce(cvec[:, :], wsib, AX.X, ALU.add).then_inc(pre_v, 1)
            dve.wait_ge(pre_v, 8)
            dve.tensor_reduce(small[:, 16:17], cvec[:, :], AX.X, ALU.add).then_inc(pre_v, 1)
            dve.wait_ge(pre_v, 9)
            dve.scalar_tensor_tensor(out=biasc[:, :], in0=small[:, 16:17].broadcast_to([P, PR]),
                                     scalar=-1.0 / PR, in1=cvec[:, :], op0=ALU.mult, op1=ALU.add
                                     ).then_inc(pre_v, 1)
            dve.wait_ge(pre_v, 10)
            dve.tensor_scalar(biasc[:, :], biasc[:, :], bscol, None, ALU.mult).then_inc(pre_v, 1)
            dve.wait_ge(pre_v, 11)

            def late(n):
                if n == 2:
                    dve.wait_ge(ld_late, 16 * 7)
                    dve.tensor_scalar(part, wz_f[:, 0, :], bq[:, 0:1], None, ALU.mult).then_inc(part_ok, 1)
                    for s in range(1, QS):
                        dve.wait_ge(part_ok, s)
                        dve.scalar_tensor_tensor(out=part, in0=wz_f[:, s, :], scalar=bq[:, s:s + 1],
                                                 in1=part, op0=ALU.mult, op1=ALU.add).then_inc(part_ok, 1)
                if n == 3:
                    dve.wait_ge(part_ok, QS)
                    dve.tensor_scalar(small[:, 17:18], gpcol, 0.5, None, ALU.mult)
                    dve.tensor_scalar(small[:, 18:19], bpcol, E / 2.0, None, ALU.mult).then_inc(late_v, 1)
                    dve.tensor_scalar(sel[:, :, :], sel[:, :, :], gpcol, None, ALU.mult).then_inc(late_v, 1)
                    dve.wait_ge(late_v, 2)
                    dve.tensor_copy(sel[:, 0, 96:97], small[:, 18:19])
                    dve.tensor_copy(sel[0:PR, 1, D:D + 1], bpcol[0:PR, :]).then_inc(late_v, 1)
                    for s in range(QS):
                        dve.tensor_scalar(wz_f[:, s, :], wz_f[:, s, :], gq[:, s:s + 1], small[:, 17:18],
                                          ALU.mult, ALU.mult)
                if n == 5:
                    dve.wait_ge(late_p, 1)
                    dve.tensor_copy(wz_f[:, QS, :], bank_h[0][:, :]).then_inc(late_v, 1)
                if n == 6:
                    dve.wait_ge(late_a, 1)
                    TT(r(wz_l[:, :, :]), wz_f[:, :, :], wz_h[:, :, :], ALU.subtract).then_inc(late_v, 1)
                    dve.wait_ge(late_a, 3)
                    TT(r(w1_l[:, :, :]), w1_f[:, :, :], w1_h[:, :, :],
                       ALU.subtract).then_inc(late_v, 1)
                    TT(r(w2_l[:, :, :]), w2_f[:, :, :], w2_h[:, :, :],
                       ALU.subtract).then_inc(late_v, 1)

            def sum_s(n, q):
                dve.wait_ge(sq_ok, 2 * n + q + 1)
                dve.tensor_reduce(ssum[:, q, :], sq[:, :, :], AX.X, ALU.add).then_inc(ssum_ok, 1)

            def scale_t(n, k, q):
                dve.wait_ge(sstd_ok, 2 * n + q + 1)
                dve.reciprocal(srs[:, q, :], sstd[:, q, :]).then_inc(srs_ok, 1)
                dve.wait_ge(srs_ok, 2 * n + q + 1)
                y = tt[:, k, 32 * q:32 * q + 32, 0:PR]
                TT(y, y, srs[:, q, :].unsqueeze(2).broadcast_to([P, 2 * GRP, PR]), ALU.mult
                   ).then_inc(t_ok, 1)

            def mixed_lo(n, q):
                dve.wait_ge(uh_ok, 2 * n + q + 1)
                TT(r(u_l[:, q, :]), bank_u[:, :], u_h[:, q, :], ALU.subtract).then_inc(ul_ok, 1)

            def add_bias(n, k, h):
                dve.wait_ge(projected, 4 * n + h + 1)
                after(dve, z_done, 2 * n - 2)
                TT(tt[:, k, GRP * h:GRP * h + GRP, 0:PR],
                   bank_y[h % 2][:, :].rearrange("p (b v) -> p b v", v=PR),
                   biasc[:, :].unsqueeze(1).broadcast_to([P, GRP, PR]), ALU.add).then_inc(y_ok, 1)

            def times_e(n, k, q):
                dve.wait_ge(grammed, 2 * n + q + 1)
                a, b = 512 * q, min(512 * (q + 1), TILES * D)
                TT(prod[:, a:b], bank_g[:, 0:b - a], emb[:, k, a:b], ALU.mult).then_inc(prod_ok, 1)

            def reduce_e(n):
                dve.wait_ge(prod_ok, 2 * n + 2)
                dve.tensor_reduce(var[:, :], prod[:, :].rearrange("p (t d) -> p t d", d=D), AX.X,
                                  ALU.add).then_inc(var_ok, 1)
                dve.wait_ge(var_ok, n + 1)
                dve.tensor_scalar(var[:, :], var[:, :], 0.0, EPS, ALU.max, ALU.add).then_inc(vclip_ok, 1)

            def scale_e(n, k):
                dve.wait_ge(std_ok, n + 1)
                dve.reciprocal(rstd[:, :], std[:, :]).then_inc(rstd_ok, 1)
                dve.wait_ge(rstd_ok, n + 1)
                e = emb[:, k, :].rearrange("p (t d) -> p t d", d=D)
                TT(e, e, rstd[:, :].unsqueeze(2).broadcast_to([P, TILES, D]), ALU.mult).then_inc(scaled, 1)

            def stats_x(m):
                dve.wait_ge(xb_ok, m + 1)
                for a in range(2):
                    ins = dve.bn_stats(xst[:, a, :], xb[:, a, :])
                ins.then_inc(xst_ok, 1)
                dve.wait_ge(ones_ok, 1)
                dve.wait_ge(xst_ok, m + 1)
                for a in range(2):
                    ins = dve.bn_aggr(xmv[:, a, :], xst[:, a, :])
                ins.then_inc(xmv_ok, 1)

            def norm_x(m):
                dve.wait_ge(xstd_ok, m + 1)
                dve.reciprocal(xrs[:, :], xstd[:, :]).then_inc(xrs_ok, 1)
                dve.wait_ge(xrs_ok, m + 1)
                for a in range(2):
                    dve.tensor_scalar(xb[:, a, :], xb[:, a, :], xmv[:, a, 0:1], xrs[:, a:a + 1],
                                      ALU.subtract, ALU.mult).then_inc(xn_ok, 1)

            def stats_h(m, a):
                dve.wait_ge(flat_done, 2 * m + a + 1)
                dve.bn_stats(hst[:, a, :], bank_h[a][:, :]).then_inc(hst_ok, 1)
                dve.wait_ge(ones_ok, 1)
                dve.wait_ge(hst_ok, 2 * m + a + 1)
                dve.bn_aggr(hmv[:, a, :], hst[:, a, :]).then_inc(hmv_ok, 1)

            def norm_h(m, a):
                dve.wait_ge(hstd_ok, 2 * m + a + 1)
                dve.reciprocal(hrs[:, a:a + 1], hstd[:, a:a + 1]).then_inc(hrs_ok, 1)
                dve.wait_ge(hrs_ok, 2 * m + a + 1)
                after(dve, znt_done, 2 * m + a - 1)
                dve.tensor_scalar(zn[:, a, :], bank_h[a][:, 0:KEEP], hmv[:, a, 0:1],
                                  hrs[:, a:a + 1], ALU.subtract, ALU.mult).then_inc(zn_ok, 1)

            def h1_lo(m):
                dve.wait_ge(h1h_ok, m + 1)
                TT(r(h1_l[:, :, :]), h1_f[:, :, :], h1_h[:, :, :], ALU.subtract).then_inc(h1l_ok, 1)

            def zt_lo(m):
                dve.wait_ge(zth_ok, m + 1)
                TT(r(zt_l[:, :, :]), zt_f[:, :, :], zt_h[:, :, :], ALU.subtract).then_inc(ztl_ok, 1)

            def dt_lo(m):
                dve.wait_ge(dth_ok, m + 1)
                TT(r(dt_l[:, :, :]), dt_f[:, :, :], dt_h[:, :, :], ALU.subtract).then_inc(dtl_ok, 1)

            def z_lo(m, a):
                dve.wait_ge(zh_ok, 2 * m + a + 1)
                TT(r(z_l[:, :, 2 * a:2 * a + 2, :]), zs[:, 2 * a:2 * a + 2].rearrange("p j s g -> p s j g"),
                   z_h[:, :, 2 * a:2 * a + 2, :], ALU.subtract).then_inc(zl_ok[a], 1)

            def body(i, blocks, supers):
                for k in range(4):
                    n = 4 * i + k
                    if blocks(n - 2):
                        scale_t(n - 2, k % 2, 0)
                        mixed_lo(n - 2, 1)
                    if blocks(n - 1):
                        reduce_e(n - 1)
                    if blocks(n - 2):
                        add_bias(n - 2, k % 2, 2)
                        add_bias(n - 2, k % 2, 3)
                    if blocks(n - 1):
                        scale_e(n - 1, (k - 1) % 4)
                    if k == 2 and supers(i - 2):
                        dt_lo(i - 2)
                    if k == 3 and supers(i - 2):
                        zt_lo(i - 2)
                    if blocks(n - 2):
                        sum_s(n - 2, 1)
                    if blocks(n):
                        times_e(n, k, 0)
                    if blocks(n - 2):
                        scale_t(n - 2, k % 2, 1)
                    if blocks(n - 1):
                        mixed_lo(n - 1, 0)
                    if k == 0 and supers(i):
                        stats_x(i)
                    if k == 1 and supers(i - 2):
                        stats_h(i - 2, 0)
                    if k == 2 and supers(i - 2):
                        stats_h(i - 2, 1)
                    if k == 3 and supers(i - 1):
                        z_lo(i - 1, 0)
                    if blocks(n - 1):
                        add_bias(n - 1, (k - 1) % 2, 0)
                        add_bias(n - 1, (k - 1) % 2, 1)
                    if k == 0 and supers(i):
                        norm_x(i)
                    if k == 0 and supers(i - 3):
                        h1_lo(i - 3)
                    if k == 1 and supers(i - 2):
                        norm_h(i - 2, 0)
                    if k == 2 and supers(i - 2):
                        norm_h(i - 2, 1)
                    if k == 3 and supers(i - 1):
                        z_lo(i - 1, 1)
                    if blocks(n - 1):
                        sum_s(n - 1, 0)
                    if blocks(n):
                        times_e(n, k, 1)
                    if isinstance(i, int):
                        late(n)

            over_supers(dve, body)


def order():
    pos = np.arange(SUP)
    return (SUP * np.arange(NSUP)[:, None] + 64 * (pos % 4) + pos // 4).reshape(-1)


def kernel(**inputs):
    import concourse.bacc as bacc
    from concourse.bass_utils import run_bass_kernel_spmd

    g = {k: np.asarray(v) for k, v in inputs.items()}
    tables = [g[f"tbl_{f}"] for f in range(NS)]
    at = order()
    row = np.arange(BLK * NS).reshape(TILES, P).T
    starts = np.concatenate([[0], np.cumsum([t.shape[0] for t in tables])[:-1]]).astype(np.int32)
    first = np.array([first_sample(t) for t in range(TILES)])
    p, q = np.meshgrid(np.arange(PR), np.arange(PR), indexing="ij")
    hi, lo = np.maximum(p, q) + 1, np.minimum(p, q) + 1
    wl = np.concatenate([g["L0_rec_Wl"], np.zeros((MAXD, 1), np.float32)], axis=1).T
    pair = np.where(p == q, wl.shape[0] - 1, hi * (hi - 1) // 2 + lo)
    wsym = wl[pair].reshape(PR, 4, QS, MAXD).transpose(1, 0, 2, 3).reshape(P, QS, MAXD)
    wx = np.zeros((P, MAXD), np.float32)
    wx[0:PR] = wl[[(v + 1) * v // 2 for v in range(PR)]]
    sel = np.zeros((P, 2, P), np.float32)
    for v in range(PR):
        sel[v::PR, 0, PR + v] = 1.0
        sel[v, 1, v] = 1.0
    dense_t = g["r_dense_t"].T
    w1 = g["W_top1"]
    w1 = np.concatenate([w1[0:KEEP], w1[MAXD:MAXD + DD]], axis=0)

    def tiles_of(w):
        return w.reshape(w.shape[0] // P, P, w.shape[1]).transpose(1, 0, 2)

    def cols(v, n):
        return v.reshape(n, P).T

    def four(v):
        return np.tile(v, 4)[:, None]

    def by_quadrant(v):
        return np.repeat(v.reshape(4, QS), PR, axis=0)

    vecs = [g["L0_rec_gs"][:, None], g["L0_rec_gd"][:, None], g["L0_rec_bd"][:, None],
            four(g["L0_rec_gsi"]), four(g["L0_rec_bsi"]), g["L0_rec_bs"][:, None],
            cols(g["L0_rec_gl"][0:KEEP], 3), cols(g["L0_rec_bl"][0:KEEP], 3),
            cols(g["b_top1"], 4), cols(g["b_top2"], 2), cols(g["W_top3"][:, 0], 2)]
    arrays = {
        "tables": np.concatenate(tables, axis=0),
        "ids": g["ids"][at].reshape(NBLK * TILES, P).T,
        "row0": starts[row % NS],
        "eye": np.eye(P, dtype=np.float32),
        "wst": g["L0_rec_Ws"].T,
        "gs": g["L0_rec_gs"],
        "vecs": np.concatenate(vecs, axis=1),
        "wdt": tiles_of(g["L0_rec_Wd"].T),
        "mixrows": g["L0_rec_Wsi"].T[row % NS],
        "mixmask": (row // NS - first[None, :])[:, :, None] == np.arange(6),
        "wsi": g["L0_rec_Wsi"],
        "wsym": wsym,
        "wx": wx,
        "gq": by_quadrant(g["L0_rec_gsi"]),
        "bq": by_quadrant(g["L0_rec_bsi"]),
        "sel": sel,
        "w1": tiles_of(w1),
        "w2": tiles_of(g["W_top2"]),
        "dense": tiles_of(dense_t),
        "dense_pos": tiles_of(dense_t[:, at]),
    }
    arrays["mixmask"] = arrays["mixmask"].astype(np.float32)
    nc = bacc.Bacc("TRN2", target_bir_lowering=False, num_devices=1)
    aps, feed = {}, {}
    for name, a in arrays.items():
        a = np.ascontiguousarray(a)
        feed[f"in_{name}"] = a
        aps[name] = nc.dram_tensor(f"in_{name}", a.shape, mybir.dt.from_np(a.dtype), kind="ExternalInput").ap()
    out = nc.dram_tensor("out_y", (1, B), F32, kind="ExternalOutput").ap()
    dlrm(nc, aps, out)
    res = run_bass_kernel_spmd(nc, [feed], core_ids=[0])
    return res.results[0]["out_y"].reshape(B, 1)
```

```python
from contextlib import ExitStack

import numpy as np

import concourse.bass as bass
from concourse import mybir

F32 = mybir.dt.float32
F32R = mybir.dt.float32r
I32 = mybir.dt.int32
ALU = mybir.AluOpType
ACT = mybir.ActivationFunctionType
AX = mybir.AxisListType

P = 128
B = 2048
NS = 26
D = 64
E = 128
PR = 32
MAXD = 512
KEEP = 384
DD = 256
H1, H2 = 512, 256
EPS = 1e-5

BLK = 64
TILES = BLK * NS // P
FIRST = 8
NBLK = B // BLK
SUP = 256
NSUP = B // SUP
GRP = 16
ZC = PR + 2
C0 = 2
LOW = PR // 2
SLOTS = 7
ROW_LO = 3
ROW_HI = 5
SPLIT = LOW * ROW_LO
QS = 8
KT1 = (KEEP + DD) // P
ROWS = sum([12500, 1250, 125000, 12500, 1000, 12500, 1000, 12500, 125000, 1000, 1000, 1000, 1000,
            125000, 12500, 1250, 1000, 1250, 1250, 12500, 12500, 1000, 12500, 1000, 1250, 1250])


def first_sample(t):
    return P * t // NS


def mix_pieces(h):
    out = []
    for t in range(GRP * NS * h // P, (GRP * NS * (h + 1) - 1) // P + 1):
        lo = max(GRP * h, first_sample(t))
        hi = min(GRP * (h + 1) - 1, (P * t + P - 1) // NS)
        out.append((t, lo, hi - lo + 1))
    return out


def dlrm(nc, x_in, out):
    with ExitStack() as ctx:
        def sb(name, shape, dt=F32):
            return ctx.enter_context(nc.sbuf_tensor(name, shape, dt))

        def ps(name):
            return ctx.enter_context(nc.psum_tensor(name, [P, 512], F32))

        def sem(name):
            return ctx.enter_context(nc.semaphore(name))

        ids = sb("ids", [P, (NBLK + 1) * TILES], I32)
        row0 = sb("row0", [P, TILES], I32)
        idx = sb("idx", [P, 4, TILES], I32)
        eye = sb("eye", [P, P])
        ones = sb("ones", [P, PR])
        epsc = sb("epsc", [P, 1])
        wt2 = sb("wt2", [P, E])
        gsb = sb("gsb", [P, E])
        wc2 = sb("wc2", [P, P])
        gram_w = sb("gram_w", [P, P])
        proj_f = sb("proj_f", [P, E])
        proj_h = sb("proj_h", [P, 2, E])
        proj_l = sb("proj_l", [P, 2, E])
        mixrows = sb("mixrows", [P, TILES, PR])
        mixmask = sb("mixmask", [P, TILES, 6])
        mix_w = sb("mix_w", [P, TILES, 6, PR])
        cvec = sb("cvec", [P, PR])
        biasc = sb("biasc", [P, PR])
        small = sb("small", [P, 24])
        vecs = sb("vecs", [P, 34])
        gscol, gdcol, bdcol, gpcol, bpcol = (vecs[:, c:c + 1] for c in range(5))
        bscol, growcol = vecs[:, 5:6], vecs[:, 20:21]
        glc, blc = vecs[:, 6:9], vecs[:, 9:12]
        b1c, b2c, w3c = vecs[:, 12:16], vecs[:, 16:18], vecs[:, 18:20]
        gq = sb("gq", [P, SLOTS])
        half = sb("half", [P, SLOTS])
        bq = sb("bq", [P, QS])
        wdt = sb("wdt", [P, 2, E])
        wz_h = sb("wz_h", [P, SLOTS, MAXD])
        wz_l = sb("wz_l", [P, SLOTS, MAXD])
        w1_h = sb("w1_h", [P, KT1, H1])
        w1_l = sb("w1_l", [P, KT1, H1])
        w2_h = sb("w2_h", [P, 4, H2])
        w2_l = sb("w2_l", [P, 4, H2])
        sel = sb("sel", [P, 4, P])
        emb = sb("emb", [P, 4, TILES * D])
        embt = sb("embt", [P, 7 * P])
        prod = sb("prod", [P, TILES * D])
        wsib = prod[:, :].rearrange("p (v n) -> p v n", n=NS)
        var = sb("var", [P, TILES])
        std = sb("std", [P, TILES])
        rstd = sb("rstd", [P, TILES])
        u_h = sb("u_h", [P, 2, 512])
        u_l = sb("u_l", [P, 2, 512])
        tt = sb("tt", [P, 2, BLK, ZC])
        sq = sb("sq", [P, 2 * GRP, PR])
        ssum = sb("ssum", [P, 2, 2 * GRP])
        sstd = sb("sstd", [P, 2, 2 * GRP])
        srs = sb("srs", [P, 2, 2 * GRP])
        zc = sb("zc", [P, 2, C0 + ZC, 32])
        zs = sb("zs", [P, 2, 4, SLOTS, 32])
        zt_f = sb("zt_f", [P, 3, SUP])
        h1_f = sb("h1_f", [P, 4, SUP])
        h2 = h1_f[:, 0:2, :]
        wx_f = h1_f[:, 0:2, :].rearrange("p c b -> p (c b)")
        zn = sb("zn", [P, 2, KEEP])
        part = zn[:, :, :].rearrange("p a k -> p (a k)")[:, 0:MAXD]
        hst = sb("hst", [P, 2, 6])
        hmv = sb("hmv", [P, 2, 2])
        hstd = sb("hstd", [P, 2])
        hrs = sb("hrs", [P, 2])
        dtx = sb("dtx", [P, 2, SUP])
        dt_f = sb("dt_f", [P, 2, SUP])
        dt_l = sb("dt_l", [P, 2, SUP])
        dt_h = sb("dt_h", [P, 2, SUP])
        xb = sb("xb", [P, 2, E])
        xs = sb("xs", [P, SUP])
        xsum = sb("xsum", [P, SUP // 4])
        xst = sb("xst", [P, 2, 6])
        xmv = sb("xmv", [P, 2, 2])
        xstd = sb("xstd", [P, 2])
        xrs = sb("xrs", [P, 2])
        yrow = sb("yrow", [1, SUP])
        with ExitStack() as staging:
            wz_f = staging.enter_context(nc.sbuf_tensor("wz_f", [P, SLOTS, MAXD], F32))
            wfull = staging.enter_context(nc.sbuf_tensor("wfull", [P, QS, MAXD], F32))
        rest = wfull[:, :, :].rearrange("p s o -> p (s o)")
        w1_f = rest[:, 0:KT1 * H1].rearrange("p (t o) -> p t o", t=KT1)
        w2_f = rest[:, KT1 * H1:KT1 * H1 + 4 * H2].rearrange("p (t o) -> p t o", t=4)
        z_h = sb("z_h", [P, 2, SLOTS, P])
        z_l = sb("z_l", [P, 2, SLOTS, P])
        zt_h, zt_l = sb("zt_h", [P, 3, SUP]), sb("zt_l", [P, 3, SUP])
        h1_h, h1_l = sb("h1_h", [P, 4, SUP]), sb("h1_l", [P, 4, SUP])

        bank_t, bank_g, bank_u = ps("bank_t"), ps("bank_g"), ps("bank_u")
        bank_y = [ps("bank_y0"), ps("bank_y1")]
        bank_z = ps("bank_z")
        bank_h, bank_m = ps("bank_h"), ps("bank_m")

        def r(ap):
            return ap.bitcast(F32R)

        ld_ids, ld_small, ld_late, ld_mlp = sem("ld_ids"), sem("ld_small"), sem("ld_late"), sem("ld_mlp")
        ids_ok, idx_ok = sem("ids_ok"), sem("idx_ok")
        first_in = [sem(f"first_in{k}") for k in range(4)]
        rows_in = [sem(f"rows_in{k}") for k in range(4)]
        pre_v, pre_p, pre_a = sem("pre_v"), sem("pre_p"), sem("pre_a")
        late_v, late_a, late_p, part_ok = sem("late_v"), sem("late_a"), sem("late_p"), sem("part_ok")
        ones_ok, gains_ok = sem("ones_ok"), sem("gains_ok")
        turned, embt_ok, grammed, prod_ok = sem("turned"), sem("embt_ok"), sem("grammed"), sem("prod_ok")
        var_ok, vclip_ok, std_ok, rstd_ok, scaled = (
            sem("var_ok"), sem("vclip_ok"), sem("std_ok"), sem("rstd_ok"), sem("scaled"))
        mixed, uh_ok, ul_ok, projected = sem("mixed"), sem("uh_ok"), sem("ul_ok"), sem("projected")
        y_ok, sq_ok, ssum_ok, sstd_ok, srs_ok, t_ok = (
            sem("y_ok"), sem("sq_ok"), sem("ssum_ok"), sem("sstd_ok"), sem("srs_ok"), sem("t_ok"))
        xcol_ok, z_done, zc_ok = sem("xcol_ok"), sem("z_done"), sem("zc_ok")
        zs_in = [sem("zs_in0"), sem("zs_in1")]
        zh_ok = [sem("zh_ok0"), sem("zh_ok1")]
        sx_ok = sem("sx_ok")
        zl_ok = [sem("zl_ok0"), sem("zl_ok1")]
        flat_done, hst_ok, hmv_ok, hstd_ok, hrs_ok, zn_ok = (
            sem("flat_done"), sem("hst_ok"), sem("hmv_ok"), sem("hstd_ok"), sem("hrs_ok"), sem("zn_ok"))
        znt_done, zt_ok, zth_ok, ztl_ok = sem("znt_done"), sem("zt_ok"), sem("zth_ok"), sem("ztl_ok")
        dt_in, dth_ok, dtl_ok = sem("dt_in"), sem("dth_ok"), sem("dtl_ok")
        top1_done, h1_ok, h1h_ok, h1l_ok = sem("top1_done"), sem("h1_ok"), sem("h1h_ok"), sem("h1l_ok")
        top2_done, h2_ok, top3_done, y_out = sem("top2_done"), sem("h2_ok"), sem("top3_done"), sem("y_out")
        dtx_in, x_done, xb_ok, xst_ok, xmv_ok, xstd_ok, xrs_ok, xn_ok, xt_done, xs_ok, sx_done = (
            sem("dtx_in"), sem("x_done"), sem("xb_ok"), sem("xst_ok"), sem("xmv_ok"), sem("xstd_ok"),
            sem("xrs_ok"), sem("xn_ok"), sem("xt_done"), sem("xs_ok"), sem("sx_done"))
        stored = sem("stored")

        N_SMALL = 9

        def after(eng, s, value):
            if not isinstance(value, int) or value > 0:
                eng.wait_ge(s, value)

        def over_supers(eng, body):
            for i in (0, 1, 2):
                body(i, lambda n: 0 <= n < NBLK, lambda m: 0 <= m < NSUP)
            with eng.Fori(3, NSUP) as i:
                body(i, lambda n: True, lambda m: True)
            for i in (NSUP, NSUP + 1, NSUP + 2):
                body(i, lambda n: 0 <= n < NBLK, lambda m: 0 <= m < NSUP)


        block = ctx.enter_context(nc.Block())

        @block.gpsimd
        def _(pool):
            def copy_indices(n, k):
                pool.tensor_copy(idx[:, k, :], ids[:, bass.ds(TILES * n, TILES)]).then_inc(idx_ok, 1)

            def body(i, blocks, supers):
                for k in range(4):
                    n = 4 * i + k
                    if not blocks(n):
                        continue
                    after(pool, mixed, 2 * n - 6)
                    if blocks(n - 3):
                        before = i if k < 3 else i + 1
                        pool.wait_ge(first_in[(k + 1) % 4], 16 * FIRST * before)
                        pool.wait_ge(rows_in[(k + 1) % 4], 16 * (TILES - FIRST) * before)
                    pool.wait_ge(idx_ok, n + 1)
                    if blocks(n + 1):
                        copy_indices(n + 1, (k + 1) % 4)
                    for t in range(TILES):
                        pool.indirect_dma_start(
                            emb[:, k, D * t:D * t + D], None, x_in["tables"],
                            bass.IndirectOffsetOnAxis(ap=idx[:, k, t:t + 1], axis=0),
                        ).then_inc(first_in[k] if t < FIRST else rows_in[k], 16)

            pool.memset(ids[:, NBLK * TILES:], 0).then_inc(ids_ok, 1)
            pool.wait_ge(ids_ok, 2)
            copy_indices(0, 0)
            over_supers(pool, body)

        @block.sync
        def _(sp):
            sp.dma_start(ids[:, 0:NBLK * TILES], x_in["ids"]).then_inc(ld_ids, 16)
            sp.dma_start(row0[:, :], x_in["row0"]).then_inc(ld_ids, 16)
            sp.dma_start(eye[:, :], x_in["eye"]).then_inc(ld_small, 16)
            sp.dma_start(wt2[0:D, :], x_in["wst"]).then_inc(ld_small, 16)
            sp.dma_start(wt2[D:P, :], x_in["wst"]).then_inc(ld_small, 16)
            sp.dma_start(gsb[:, :], x_in["gs"].partition_broadcast(P)).then_inc(ld_small, 16)
            sp.dma_start(vecs[:, 0:21], x_in["vecs"]).then_inc(ld_small, 16)
            sp.dma_start(wdt[:, :, :], x_in["wdt"]).then_inc(ld_small, 16)
            sp.dma_start(mixrows[:, :, :], x_in["mixrows"]).then_inc(ld_small, 16)
            sp.dma_start(mixmask[:, :, :], x_in["mixmask"]).then_inc(ld_small, 16)
            sp.dma_start(wsib, x_in["wsi"].partition_broadcast(P)).then_inc(ld_small, 16)
            sp.dma_start(wfull[:, :, :], x_in["wfull"]).then_inc(ld_late, 16)
            sp.dma_start(bq[:, :], x_in["bq"]).then_inc(ld_late, 16)
            sp.dma_start(wz_f[:, :, :], x_in["wrows"]).then_inc(ld_late, 16)
            sp.dma_start(gq[:, :], x_in["gq"]).then_inc(ld_late, 16)
            sp.dma_start(half[:, :], x_in["half"]).then_inc(ld_late, 16)
            sp.dma_start(wx_f, x_in["wx"]).then_inc(ld_late, 16)
            sp.dma_start(sel[:, :, :], x_in["sel"]).then_inc(ld_late, 16)

            def move_products(m, h):
                sp.wait_ge(zc_ok, 8 * m + 4 * h + 4)
                after(sp, zl_ok[h], m)
                for j in range(4):
                    low, high = PR * j, PR * j + LOW
                    sp.dma_start(zs[0:SPLIT, h, j], zc[low:low + LOW, h, 0:ROW_LO * SLOTS]
                                 ).then_inc(zs_in[h], 16)
                    sp.dma_start(zs[SPLIT:P, h, j], zc[high:high + LOW, h, 1:1 + ROW_HI * SLOTS]
                                 ).then_inc(zs_in[h], 16)

            def body(i, blocks, supers):
                if supers(i):
                    after(sp, x_done, i)
                    sp.dma_start(dtx[:, :, :], x_in["dense_pos"][:, :, bass.ds(SUP * i, SUP)]
                                 ).then_inc(dtx_in, 16)
                if isinstance(i, int) and i == 0:
                    sp.wait_ge(part_ok, QS)
                    sp.dma_start(w1_f, x_in["w1"]).then_inc(ld_mlp, 16)
                    sp.dma_start(w2_f, x_in["w2"]).then_inc(ld_mlp, 16)
                if supers(i - 1):
                    after(sp, dtl_ok, i - 1)
                    sp.dma_start(dt_f[:, :, :], x_in["dense"][:, :, bass.ds(SUP * i - SUP, SUP)]
                                 ).then_inc(dt_in, 16)
                    move_products(i - 1, 0)
                    move_products(i - 1, 1)

            over_supers(sp, body)
            sp.wait_ge(stored, 16 * NSUP)

        @block.tensor
        def _(pe):
            pe.wait_ge(pre_v, 3)
            pe.transpose(bank_t[:, 0:P], wt2[:, :], eye[:, :]).then_inc(pre_p, 1)
            pe.wait_ge(pre_a, 1)
            pe.matmul(bank_g[:, 0:D], wc2[:, :], wc2[:, 0:D], start=True, stop=True).then_inc(pre_p, 1)
            pe.wait_ge(pre_a, 3)
            pe.wait_ge(pre_v, 11)

            def turn(i, n, k, q):
                if q == 0:
                    pe.wait_ge(first_in[k], 16 * FIRST * (i + 1))
                else:
                    pe.wait_ge(rows_in[k], 16 * (TILES - FIRST) * (i + 1))
                after(pe, embt_ok, 2 * n + q)
                for c in range(4 * q, 4 + 3 * q):
                    t0 = min(2 * c, TILES - 2)
                    mm = pe.transpose(bank_t[:, P * (c - 4 * q):P * (c - 4 * q) + P],
                                      emb[:, k, D * t0:D * t0 + P], eye[:, :])
                mm.then_inc(turned, 1)

            def gram(n, q):
                pe.wait_ge(embt_ok, 2 * n + q + 1)
                after(pe, prod_ok, 2 * n + q)
                for c in range(4 * q, 4 + 3 * q):
                    whole = c < 6
                    o = P * (c - 4 * q)
                    mm = pe.matmul(bank_g[:, o:o + (P if whole else D)], embt[:, P * c:P * c + P],
                                   gram_w[:, 0 if whole else D:P], start=True, stop=True)
                mm.then_inc(grammed, 1)

            def mix(n, k, q):
                pe.wait_ge(scaled, 2 * n + q + 1)
                after(pe, ul_ok, 2 * n + q)
                for a in range(2):
                    h = 2 * q + a
                    pieces = mix_pieces(h)
                    for c, (t, lo, cnt) in enumerate(pieces):
                        o = PR * (lo - GRP * h)
                        w0 = PR * (lo - first_sample(t))
                        mm = pe.matmul(
                            bank_u[D * a:D * a + D, o:o + PR * cnt], emb[:, k, D * t:D * t + D],
                            mix_w[:, t, :, :].rearrange("p s v -> p (s v)")[:, w0:w0 + PR * cnt],
                            start=(c == 0), stop=(c == len(pieces) - 1), skip_group_check=True)
                mm.then_inc(mixed, 1)

            def project(n, h):
                q, a = h // 2, h % 2
                pe.wait_ge(ul_ok, 2 * n + q + 1)
                after(pe, y_ok, 4 * n + h - 1)
                y = bank_y[a][:, :]
                pe.matmul(y, r(proj_h[:, a, :]), r(u_h[:, q, :]), start=True, stop=False)
                pe.matmul(y, r(proj_l[:, a, :]), r(u_h[:, q, :]), start=False, stop=False)
                pe.matmul(y, r(proj_h[:, a, :]), r(u_l[:, q, :]), start=False, stop=True
                          ).then_inc(projected, 1)

            def products(n, k, q):
                pe.wait_ge(t_ok, 2 * n + q + 1)
                pe.wait_ge(xcol_ok, n + 1)
                after(pe, zc_ok, 2 * n + q)
                for g in range(8):
                    for j in range(4):
                        b = 32 * q + 4 * g + j
                        mm = pe.matmul(bank_z[PR * j:PR * j + PR, ZC * g:ZC * g + ZC],
                                       tt[:, k, b, ZC - PR:ZC], tt[:, k, b, :], start=True, stop=True)
                mm.then_inc(z_done, 1)

            def flat(m, a, slots):
                if slots[0] == 0:
                    pe.wait_ge(zl_ok[a], m + 1)
                    after(pe, zt_ok, 2 * m + a)
                for s in slots:
                    zh, zl = z_h[:, a, s, :], z_l[:, a, s, :]
                    pe.matmul(bank_h[:, :], r(zh), r(wz_h[:, s, :]), start=(s == 0), stop=False)
                    pe.matmul(bank_h[:, :], r(zh), r(wz_l[:, s, :]), start=False, stop=False)
                    mm = pe.matmul(bank_h[:, :], r(zl), r(wz_h[:, s, :]), start=False,
                                   stop=(s == SLOTS - 1))
                if slots[-1] == SLOTS - 1:
                    mm.then_inc(flat_done, 1)

            def turn_z(m, a):
                pe.wait_ge(zn_ok, 2 * m + a + 1)
                for c in range(3):
                    mm = pe.transpose(bank_h[:, P * c:P * c + P], zn[:, a, P * c:P * c + P], eye[:, :])
                mm.then_inc(znt_done, 1)

            def top1(m, c):
                if c == 0:
                    pe.wait_ge(dtl_ok, m + 1)
                    after(pe, y_out, m)
                if c == 2:
                    pe.wait_ge(h1_ok, 2 * m + 1)
                o = bank_m[:, SUP * (c % 2):SUP * (c % 2) + SUP]
                w = slice(P * c, P * c + P)
                for t in (3, 4, 0, 1, 2):
                    if c == 0 and t == 0:
                        pe.wait_ge(ztl_ok, 2 * m + 2)
                    hi = zt_h[:, t, :] if t < 3 else dt_h[:, t - 3, :]
                    lo = zt_l[:, t, :] if t < 3 else dt_l[:, t - 3, :]
                    pe.matmul(o, r(w1_h[:, t, w]), r(hi), start=(t == 3), stop=False)
                    pe.matmul(o, r(w1_l[:, t, w]), r(hi), start=False, stop=False)
                    mm = pe.matmul(o, r(w1_h[:, t, w]), r(lo), start=False, stop=(t == 2))
                if c % 2:
                    mm.then_inc(top1_done, 1)

            def top2(m):
                pe.wait_ge(h1l_ok, 2 * m + 2)
                for c in range(2):
                    o = bank_m[:, SUP * c:SUP * c + SUP]
                    w = slice(P * c, P * c + P)
                    for t in range(4):
                        pe.matmul(o, r(w2_h[:, t, w]), r(h1_h[:, t, :]), start=(t == 0), stop=False)
                        pe.matmul(o, r(w2_l[:, t, w]), r(h1_h[:, t, :]), start=False, stop=False)
                        mm = pe.matmul(o, r(w2_h[:, t, w]), r(h1_l[:, t, :]), start=False, stop=(t == 3))
                mm.then_inc(top2_done, 1)

            def top3(m):
                pe.wait_ge(h2_ok, m + 1)
                for c in range(2):
                    mm = pe.matmul(bank_m[0:1, 0:SUP], w3c[:, c:c + 1], h2[:, c, :],
                                   start=(c == 0), stop=(c == 1))
                mm.then_inc(top3_done, 1)

            def dense_x(m, n):
                pe.wait_ge(dtx_in, 16 * (m + 1))
                pe.wait_ge(embt_ok, 2 * n + 1)
                for a in range(2):
                    for c in range(2):
                        mm = pe.matmul(bank_t[:, E * a:E * a + E], dtx[:, c, P * a:P * a + P],
                                       wdt[:, c, :], start=(c == 0), stop=(c == 1))
                mm.then_inc(x_done, 1)

            def turn_x(m, n):
                pe.wait_ge(xn_ok, 2 * m + 2)
                pe.wait_ge(embt_ok, 2 * n + 2)
                for a in range(2):
                    mm = pe.transpose(bank_t[:, P * a:P * a + P], xb[:, a, :], eye[:, :])
                mm.then_inc(xt_done, 1)

            def sum_x(m, n):
                pe.wait_ge(xs_ok, m + 1)
                pe.wait_ge(embt_ok, 2 * n + 1)
                for j in range(4):
                    mm = pe.matmul(bank_t[PR * j:PR * j + PR, 0:SUP // 4], ones[:, :],
                                   xs[:, :].rearrange("p (g j) -> p j g", j=4)[:, j, :],
                                   start=True, stop=True)
                mm.then_inc(sx_done, 1)

            def late(n):
                if n == 1:
                    pe.wait_ge(late_v, 2)
                    pe.matmul(bank_h[:, :], sel[:, 0, :], part, start=True, stop=True)
                    pe.matmul(bank_m[:, :], sel[:, 1, :], part, start=True, stop=True).then_inc(late_p, 1)
                if n == 2:
                    pe.wait_ge(late_v, 3)
                    pe.matmul(bank_h[:, :], sel[:, 2, :], part, start=True, stop=True)
                    pe.matmul(bank_m[:, :], sel[:, 3, :], wx_f, start=True, stop=True).then_inc(late_p, 1)
                if n == 6:
                    pe.wait_ge(late_v, 5)
                if n == 7:
                    pe.wait_ge(late_v, 7)

            def body(i, blocks, supers):
                for k in range(4):
                    n = 4 * i + k
                    if isinstance(i, int):
                        late(n)
                    if blocks(n - 2):
                        project(n - 2, 0)
                        project(n - 2, 1)
                    if blocks(n):
                        if k == 2 and supers(i):
                            pe.wait_ge(xs_ok, i + 1)
                        turn(i, n, k, 0)
                    if blocks(n - 2):
                        mix(n - 2, (k - 2) % 4, 1)
                    if blocks(n):
                        gram(n, 0)
                    if blocks(n - 3):
                        products(n - 3, (k - 3) % 2, 1)
                    if k == 0 and supers(i):
                        dense_x(i, n)
                    if k == 0 and supers(i - 2):
                        flat(i - 2, 1, range(4, SLOTS))
                    if k == 1 and supers(i - 1):
                        flat(i - 1, 0, range(0, 3))
                    if k == 1 and supers(i - 3):
                        top3(i - 3)
                    if k == 2 and supers(i):
                        sum_x(i, n)
                    if k == 2 and supers(i - 1):
                        flat(i - 1, 0, range(3, SLOTS))
                    if k == 3 and supers(i - 2):
                        top1(i - 2, 3)
                    if blocks(n - 2):
                        project(n - 2, 2)
                        project(n - 2, 3)
                    if blocks(n):
                        if k == 0 and supers(i):
                            pe.wait_ge(xb_ok, i + 1)
                        if k == 2 and supers(i):
                            pe.wait_ge(sx_ok, i + 1)
                        turn(i, n, k, 1)
                    if blocks(n - 1):
                        mix(n - 1, (k - 1) % 4, 0)
                    if blocks(n):
                        gram(n, 1)
                    if blocks(n - 2):
                        products(n - 2, k % 2, 0)
                    if k == 0 and supers(i - 3):
                        top2(i - 3)
                    if k == 0 and supers(i - 2):
                        turn_z(i - 2, 1)
                    if k == 1 and supers(i - 2):
                        top1(i - 2, 0)
                    if k == 1 and supers(i):
                        turn_x(i, n)
                    if k == 1 and supers(i - 2):
                        top1(i - 2, 1)
                    if k == 2 and supers(i - 2):
                        top1(i - 2, 2)
                    if k == 2 and supers(i - 1):
                        turn_z(i - 1, 0)
                    if k == 3 and supers(i - 1):
                        flat(i - 1, 1, range(0, 4))

            over_supers(pe, body)

        @block.scalar
        def _(act):
            A = nc.scalar.activation
            act.wait_ge(pre_p, 1)
            act.copy(wc2[:, :], bank_t[:, 0:P]).then_inc(pre_a, 1)
            act.wait_ge(pre_p, 2)
            act.wait_ge(pre_v, 4)
            act.mul(gram_w[0:D, 0:D], bank_g[0:D, 0:D], 1.0 / E).then_inc(pre_a, 1)
            act.mul(gram_w[D:P, D:P], bank_g[D:P, 0:D], 1.0 / E).then_inc(pre_a, 1)

            def rows_out(n, q):
                act.wait_ge(turned, 2 * n + q + 1)
                after(act, grammed, 2 * n + q - 1)
                w = P * (4 - q)
                act.copy(embt[:, 512 * q:512 * q + w], bank_t[:, 0:w]).then_inc(embt_ok, 1)

            def products_out(m, n, k, q):
                act.wait_ge(z_done, 2 * n + q + 1)
                half = k // 2
                after(act, zs_in[half], 8 * 16 * m)
                g0 = 16 * (k % 2) + 8 * q
                act.copy(zc[:, half, C0:, g0:g0 + 8],
                         bank_z[:, 0:8 * ZC].rearrange("p (g c) -> p c g", c=ZC)).then_inc(zc_ok, 1)

            def mixed_hi(n, q):
                act.wait_ge(mixed, 2 * n + q + 1)
                after(act, projected, 4 * n + 2 * q - 2)
                act.copy(r(u_h[:, q, :]), bank_u[:, :]).then_inc(uh_ok, 1)

            def squares(n, k, q):
                act.wait_ge(y_ok, 4 * n + 2 * q + 2)
                after(act, ssum_ok, 2 * n + q)
                A(sq[:, :, :], tt[:, k, 32 * q:32 * q + 32, ZC - PR:ZC], ACT.Square).then_inc(sq_ok, 1)

            def root_s(n, q):
                act.wait_ge(ssum_ok, 2 * n + q + 1)
                A(sstd[:, q, :], ssum[:, q, :], ACT.Sqrt, bias=epsc[:, 0:1], scale=1.0 / PR
                  ).then_inc(sstd_ok, 1)

            def xcol(m, n, k, part4):
                act.wait_ge(xs_ok, m + 1)
                after(act, z_done, 2 * n - 2)
                act.copy(tt[:, k, :, 0], xs[:, BLK * part4:BLK * part4 + BLK]).then_inc(xcol_ok, 1)

            def relu1(m, pair):
                act.wait_ge(top1_done, 2 * m + pair + 1)
                if pair == 0:
                    after(act, top3_done, m)
                for c in (2 * pair, 2 * pair + 1):
                    ins = A(h1_f[:, c, :], bank_m[:, SUP * (c % 2):SUP * (c % 2) + SUP],
                            ACT.Relu, bias=b1c[:, c:c + 1])
                ins.then_inc(h1_ok, 1)

            def h1_hi(m, pair):
                act.wait_ge(h1_ok, 2 * m + pair + 1)
                after(act, top2_done, m)
                c = slice(2 * pair, 2 * pair + 2)
                act.copy(r(h1_h[:, c, :]), h1_f[:, c, :]).then_inc(h1h_ok, 1)

            def relu2(m):
                act.wait_ge(top2_done, m + 1)
                for c in range(2):
                    ins = A(h2[:, c, :], bank_m[:, SUP * c:SUP * c + SUP], ACT.Relu,
                            bias=b2c[:, c:c + 1])
                ins.then_inc(h2_ok, 1)

            def store_y(m):
                act.wait_ge(top3_done, m + 1)
                after(act, stored, 16 * m)
                act.copy(yrow[:, :], bank_m[0:1, 0:SUP]).then_inc(y_out, 1)
                act.wait_ge(y_out, m + 1)
                act.dma_start(out[:, bass.ds(SUP * m, SUP)], yrow[:, :]).then_inc(stored, 16)

            def root_h(m, a):
                act.wait_ge(hmv_ok, 2 * m + a + 1)
                A(hstd[:, a:a + 1], hmv[:, a, 1:2], ACT.Sqrt, bias=epsc[:, 0:1]).then_inc(hstd_ok, 1)

            def gains_z(m, a):
                act.wait_ge(znt_done, 2 * m + a + 1)
                if a == 0:
                    after(act, ztl_ok, 2 * m)
                for c in range(3):
                    ins = A(zt_f[:, c, P * a:P * a + P], bank_h[:, P * c:P * c + P], ACT.Identity,
                            scale=glc[:, c:c + 1], bias=blc[:, c:c + 1])
                ins.then_inc(zt_ok, 1)

            def zt_hi(m, a):
                act.wait_ge(zt_ok, 2 * m + a + 1)
                after(act, top1_done, 2 * m)
                part_a = slice(P * a, P * a + P)
                act.copy(r(zt_h[:, :, part_a]), zt_f[:, :, part_a]).then_inc(zth_ok, 1)

            def dt_hi(m):
                act.wait_ge(dt_in, 16 * (m + 1))
                after(act, top1_done, 2 * m)
                act.copy(r(dt_h[:, :, :]), dt_f[:, :, :]).then_inc(dth_ok, 1)

            def z_hi(m, a):
                if isinstance(m, int) and m == 0 and a == 0:
                    act.wait_ge(late_v, 5)
                act.wait_ge(zs_in[a], 8 * 16 * (m + 1))
                after(act, flat_done, 2 * m + a - 1)
                act.copy(r(z_h[:, a, :, :].rearrange("p s (j g) -> p s j g", j=4)),
                         zs[:, a].rearrange("p j s g -> p s j g")).then_inc(zh_ok[a], 1)

            def x_out(m):
                act.wait_ge(x_done, m + 1)
                after(act, xt_done, m)
                act.copy(xb[:, :, :].rearrange("p a e -> p (a e)"), bank_t[:, 0:2 * E]).then_inc(xb_ok, 1)

            def root_x(m):
                act.wait_ge(xmv_ok, m + 1)
                A(xstd[:, :], xmv[:, :, 1], ACT.Sqrt, bias=epsc[:, 0:1]).then_inc(xstd_ok, 1)

            def gains_x(m):
                act.wait_ge(xt_done, m + 1)
                after(act, sx_done, m)
                after(act, xcol_ok, 4 * m)
                A(xs[:, :], bank_t[:, 0:SUP], ACT.Identity, scale=gdcol, bias=bdcol).then_inc(xs_ok, 1)

            def sum_x_out(m):
                act.wait_ge(sx_done, m + 1)
                act.copy(xsum[:, :], bank_t[:, 0:SUP // 4]).then_inc(sx_ok, 1)

            def place_sum_x(m):
                act.wait_ge(sx_ok, m + 1)
                after(act, zs_in[1], 8 * 16 * m)
                act.copy(zc[:, :, 0, :], xsum[:, :].rearrange("p (h g) -> p h g", h=2))

            def root_e(n):
                act.wait_ge(vclip_ok, n + 1)
                A(std[:, :], var[:, :], ACT.Sqrt).then_inc(std_ok, 1)

            def scale_e(n, k, tiles):
                act.wait_ge(rstd_ok, n + 1)
                for t in tiles:
                    ins = act.mul(emb[:, k, D * t:D * t + D], emb[:, k, D * t:D * t + D], rstd[:, t:t + 1])
                if tiles[-1] in (6, TILES - 1):
                    ins.then_inc(scaled, 1)

            def late(n):
                if n == 3:
                    act.wait_ge(late_v, 4)
                    act.copy(r(wz_h[:, :, :]), wz_f[:, :, :]).then_inc(late_a, 1)
                if n == 5:
                    act.wait_ge(ld_mlp, 32)
                    act.copy(r(w1_h[:, :, :]), w1_f).then_inc(late_a, 1)
                    act.copy(r(w2_h[:, :, :]), w2_f).then_inc(late_a, 1)
                if n == 7:
                    act.wait_ge(late_v, 7)

            def body(i, blocks, supers):
                for k in range(4):
                    n = 4 * i + k
                    m2 = i - 1 if k < 2 else i
                    m3 = i - 1 if k < 3 else i
                    if isinstance(i, int):
                        late(n)
                    if blocks(n - 1):
                        root_e(n - 1)
                    if blocks(n - 2):
                        xcol(m2, n - 2, k % 2, (k - 2) % 4)
                    if blocks(n):
                        rows_out(n, 0)
                    if blocks(n - 2):
                        mixed_hi(n - 2, 1)
                    if k == 1 and supers(i - 3):
                        relu2(i - 3)
                    if k == 1 and supers(i - 2):
                        gains_z(i - 2, 1)
                        zt_hi(i - 2, 1)
                    if blocks(n - 2):
                        squares(n - 2, k % 2, 0)
                    if blocks(n - 3):
                        products_out(m3, n - 3, (k - 3) % 4, 1)
                    if blocks(n - 1):
                        scale_e(n - 1, (k - 1) % 4, range(0, 7))
                    if blocks(n - 2):
                        root_s(n - 2, 0)
                    if k == 0 and supers(i):
                        x_out(i)
                    if k == 2 and supers(i - 2):
                        relu1(i - 2, 0)
                        h1_hi(i - 2, 0)
                    if k == 3 and supers(i):
                        place_sum_x(i)
                    if k == 3 and supers(i - 1):
                        gains_z(i - 1, 0)
                    if k == 2 and supers(i):
                        sum_x_out(i)
                    if blocks(n):
                        rows_out(n, 1)
                    if blocks(n - 1):
                        mixed_hi(n - 1, 0)
                    if k == 1 and supers(i - 3):
                        store_y(i - 3)
                    if k == 0 and supers(i - 2):
                        root_h(i - 2, 1)
                    if k == 2 and supers(i - 1):
                        root_h(i - 1, 0)
                    if k == 1 and supers(i):
                        root_x(i)
                    if blocks(n - 2):
                        squares(n - 2, k % 2, 1)
                        products_out(m2, n - 2, (k - 2) % 4, 0)
                    if blocks(n - 1):
                        scale_e(n - 1, (k - 1) % 4, range(7, TILES))
                    if blocks(n - 2):
                        root_s(n - 2, 1)
                    if k == 1 and supers(i):
                        gains_x(i)
                    if k == 0 and supers(i - 2):
                        zt_hi(i - 2, 0)
                    if k == 0 and supers(i - 1):
                        z_hi(i - 1, 0)
                    if k == 2 and supers(i - 1):
                        z_hi(i - 1, 1)
                    if k == 3 and supers(i - 1):
                        dt_hi(i - 1)
                    if k == 3 and supers(i - 2):
                        relu1(i - 2, 1)
                        h1_hi(i - 2, 1)

            act.wait_ge(pre_v, 11)
            over_supers(act, body)

        @block.vector
        def _(dve):
            TT = dve.tensor_tensor
            dve.memset(epsc[:, :], EPS)
            dve.memset(ones[:, :], 1.0)
            dve.memset(gram_w[:, :], 0.0)
            dve.memset(proj_h[:, :, :], 0.0)
            dve.memset(proj_l[:, :, :], 0.0)
            dve.memset(zc[:, :, 1, :], 1.0)
            dve.memset(tt[:, :, :, 1:2], 1.0).then_inc(ones_ok, 1)
            dve.wait_ge(ld_ids, 32)
            drawn = ids[:, 0:NBLK * TILES].rearrange("p (b t) -> p b t", t=TILES)
            TT(drawn, drawn,
               row0[:, :].unsqueeze(1).broadcast_to([P, NBLK, TILES]), ALU.add).then_inc(ids_ok, 1)
            dve.wait_ge(ld_small, 16 * N_SMALL)
            dve.wait_ge(ones_ok, 1)
            dve.tensor_reduce(small[:, 0:1], wt2[:, :], AX.X, ALU.add).then_inc(pre_v, 1)
            dve.wait_ge(pre_v, 1)
            dve.tensor_scalar(small[:, 1:2], small[:, 0:1], 1.0 / E, None, ALU.mult).then_inc(pre_v, 1)
            dve.wait_ge(pre_v, 2)
            dve.tensor_scalar(wt2[:, :], wt2[:, :], small[:, 1:2], None, ALU.subtract).then_inc(pre_v, 1)
            dve.wait_ge(pre_v, 3)
            TT(proj_f[:, :], wt2[:, :], gsb[:, :], ALU.mult).then_inc(pre_v, 1)
            dve.wait_ge(pre_v, 4)
            for a in range(2):
                s = slice(D * a, D * a + D)
                ins = dve.tensor_copy(r(proj_h[s, a, :]), proj_f[s, :])
            ins.then_inc(pre_v, 1)
            dve.wait_ge(pre_v, 5)
            for a in range(2):
                s = slice(D * a, D * a + D)
                TT(r(proj_l[s, a, :]), proj_f[s, :], proj_h[s, a, :], ALU.subtract)
            dve.tensor_reduce(small[:, 2:2 + TILES], mixrows[:, :, :], AX.X, ALU.add).then_inc(pre_v, 1)
            dve.wait_ge(pre_v, 6)
            dve.scalar_tensor_tensor(out=mixrows[:, :, :],
                                     in0=small[:, 2:2 + TILES].unsqueeze(2).broadcast_to([P, TILES, PR]),
                                     scalar=-1.0 / PR, in1=mixrows[:, :, :], op0=ALU.mult, op1=ALU.add
                                     ).then_inc(pre_v, 1)
            dve.wait_ge(pre_v, 7)
            for s in range(6):
                TT(mix_w[:, :, s, :], mixrows[:, :, :],
                   mixmask[:, :, s:s + 1].broadcast_to([P, TILES, PR]), ALU.mult)
            dve.tensor_reduce(cvec[:, :], wsib, AX.X, ALU.add).then_inc(pre_v, 1)
            dve.wait_ge(pre_v, 8)
            dve.tensor_reduce(small[:, 16:17], cvec[:, :], AX.X, ALU.add).then_inc(pre_v, 1)
            dve.wait_ge(pre_v, 9)
            dve.scalar_tensor_tensor(out=biasc[:, :], in0=small[:, 16:17].broadcast_to([P, PR]),
                                     scalar=-1.0 / PR, in1=cvec[:, :], op0=ALU.mult, op1=ALU.add
                                     ).then_inc(pre_v, 1)
            dve.wait_ge(pre_v, 10)
            dve.tensor_scalar(biasc[:, :], biasc[:, :], bscol, None, ALU.mult).then_inc(pre_v, 1)
            dve.wait_ge(pre_v, 11)

            dve.wait_ge(ld_late, 16 * 7)
            dve.tensor_scalar(part, wfull[:, 0, :], bq[:, 0:1], None, ALU.mult).then_inc(part_ok, 1)
            for s in range(1, QS):
                dve.wait_ge(part_ok, s)
                dve.scalar_tensor_tensor(out=part, in0=wfull[:, s, :], scalar=bq[:, s:s + 1],
                                         in1=part, op0=ALU.mult, op1=ALU.add).then_inc(part_ok, 1)
            dve.tensor_scalar(small[:, 18:19], bpcol, E / 2.0, None, ALU.mult)
            dve.tensor_scalar(sel[:, 0:2, :], sel[:, 0:2, :], gpcol, None, ALU.mult)
            dve.tensor_scalar(sel[:, 3, :], sel[:, 3, :], bpcol, None, ALU.mult)
            TT(gq[:, :], gq[:, :], half[:, :], ALU.mult).then_inc(late_v, 1)
            dve.wait_ge(late_v, 1)
            dve.tensor_scalar(sel[:, 2, :], sel[:, 2, :], small[:, 18:19], None, ALU.mult)
            dve.wait_ge(part_ok, QS)
            dve.tensor_scalar(gq[:, :], gq[:, :], growcol, None, ALU.mult).then_inc(late_v, 1)

            def late(n):
                if n == 0:
                    dve.wait_ge(late_v, 2)
                    for s in range(SLOTS):
                        ins = dve.tensor_scalar(wz_f[:, s, :], wz_f[:, s, :], gq[:, s:s + 1], None, ALU.mult)
                    ins.then_inc(gains_ok, 1)
                if n == 1:
                    dve.wait_ge(gains_ok, 1)
                    dve.wait_ge(late_p, 1)
                    TT(wz_f[:, 2, :], wz_f[:, 2, :], bank_h[:, :], ALU.add)
                    TT(wz_f[:, 3, :], wz_f[:, 3, :], bank_m[:, :], ALU.add).then_inc(late_v, 1)
                if n == 2:
                    dve.wait_ge(late_p, 2)
                    TT(wz_f[:, 1, :], wz_f[:, 1, :], bank_h[:, :], ALU.add)
                    TT(wz_f[:, 0, :], wz_f[:, 0, :], bank_m[:, :], ALU.add).then_inc(late_v, 1)
                if n in (3, 4):
                    dve.wait_ge(late_a, 1)
                    some = slice(0, 4) if n == 3 else slice(4, SLOTS)
                    ins = TT(r(wz_l[:, some, :]), wz_f[:, some, :], wz_h[:, some, :], ALU.subtract)
                    if n == 4:
                        ins.then_inc(late_v, 1)
                if n == 5:
                    dve.wait_ge(late_a, 3)
                    TT(r(w1_l[:, :, :]), w1_f, w1_h[:, :, :], ALU.subtract).then_inc(late_v, 1)
                if n == 6:
                    TT(r(w2_l[:, :, :]), w2_f, w2_h[:, :, :], ALU.subtract).then_inc(late_v, 1)

            def sum_s(n, q):
                dve.wait_ge(sq_ok, 2 * n + q + 1)
                dve.tensor_reduce(ssum[:, q, :], sq[:, :, :], AX.X, ALU.add).then_inc(ssum_ok, 1)

            def scale_t(n, k, q):
                dve.wait_ge(sstd_ok, 2 * n + q + 1)
                dve.reciprocal(srs[:, q, :], sstd[:, q, :]).then_inc(srs_ok, 1)
                dve.wait_ge(srs_ok, 2 * n + q + 1)
                y = tt[:, k, 32 * q:32 * q + 32, ZC - PR:ZC]
                TT(y, y, srs[:, q, :].unsqueeze(2).broadcast_to([P, 2 * GRP, PR]), ALU.mult
                   ).then_inc(t_ok, 1)

            def mixed_lo(n, q):
                dve.wait_ge(uh_ok, 2 * n + q + 1)
                TT(r(u_l[:, q, :]), bank_u[:, :], u_h[:, q, :], ALU.subtract).then_inc(ul_ok, 1)

            def add_bias(n, k, h):
                dve.wait_ge(projected, 4 * n + h + 1)
                after(dve, z_done, 2 * n - 2)
                TT(tt[:, k, GRP * h:GRP * h + GRP, ZC - PR:ZC],
                   bank_y[h % 2][:, :].rearrange("p (b v) -> p b v", v=PR),
                   biasc[:, :].unsqueeze(1).broadcast_to([P, GRP, PR]), ALU.add).then_inc(y_ok, 1)

            def times_e(n, k, q):
                dve.wait_ge(grammed, 2 * n + q + 1)
                a, b = 512 * q, min(512 * (q + 1), TILES * D)
                TT(prod[:, a:b], bank_g[:, 0:b - a], emb[:, k, a:b], ALU.mult).then_inc(prod_ok, 1)

            def reduce_e(n):
                dve.wait_ge(prod_ok, 2 * n + 2)
                dve.tensor_reduce(var[:, :], prod[:, :].rearrange("p (t d) -> p t d", d=D), AX.X,
                                  ALU.add).then_inc(var_ok, 1)
                dve.wait_ge(var_ok, n + 1)
                dve.tensor_scalar(var[:, :], var[:, :], 0.0, EPS, ALU.max, ALU.add).then_inc(vclip_ok, 1)

            def inverse_e(n):
                dve.wait_ge(std_ok, n + 1)
                dve.reciprocal(rstd[:, :], std[:, :]).then_inc(rstd_ok, 1)

            def stats_x(m):
                dve.wait_ge(xb_ok, m + 1)
                for a in range(2):
                    ins = dve.bn_stats(xst[:, a, :], xb[:, a, :])
                ins.then_inc(xst_ok, 1)
                dve.wait_ge(ones_ok, 1)
                dve.wait_ge(xst_ok, m + 1)
                for a in range(2):
                    ins = dve.bn_aggr(xmv[:, a, :], xst[:, a, :])
                ins.then_inc(xmv_ok, 1)

            def norm_x(m):
                dve.wait_ge(xstd_ok, m + 1)
                dve.reciprocal(xrs[:, :], xstd[:, :]).then_inc(xrs_ok, 1)
                dve.wait_ge(xrs_ok, m + 1)
                for a in range(2):
                    dve.tensor_scalar(xb[:, a, :], xb[:, a, :], xmv[:, a, 0:1], xrs[:, a:a + 1],
                                      ALU.subtract, ALU.mult).then_inc(xn_ok, 1)

            def stats_h(m, a):
                dve.wait_ge(flat_done, 2 * m + a + 1)
                dve.bn_stats(hst[:, a, :], bank_h[:, :]).then_inc(hst_ok, 1)
                dve.wait_ge(ones_ok, 1)
                dve.wait_ge(hst_ok, 2 * m + a + 1)
                dve.bn_aggr(hmv[:, a, :], hst[:, a, :]).then_inc(hmv_ok, 1)

            def norm_h(m, a):
                dve.wait_ge(hstd_ok, 2 * m + a + 1)
                dve.reciprocal(hrs[:, a:a + 1], hstd[:, a:a + 1]).then_inc(hrs_ok, 1)
                dve.wait_ge(hrs_ok, 2 * m + a + 1)
                after(dve, znt_done, 2 * m + a - 1)
                dve.tensor_scalar(zn[:, a, :], bank_h[:, 0:KEEP], hmv[:, a, 0:1],
                                  hrs[:, a:a + 1], ALU.subtract, ALU.mult).then_inc(zn_ok, 1)

            def h1_lo(m, pair):
                dve.wait_ge(h1h_ok, 2 * m + pair + 1)
                c = slice(2 * pair, 2 * pair + 2)
                TT(r(h1_l[:, c, :]), h1_f[:, c, :], h1_h[:, c, :], ALU.subtract).then_inc(h1l_ok, 1)

            def zt_lo(m, a):
                dve.wait_ge(zth_ok, 2 * m + a + 1)
                part_a = slice(P * a, P * a + P)
                TT(r(zt_l[:, :, part_a]), zt_f[:, :, part_a], zt_h[:, :, part_a], ALU.subtract
                   ).then_inc(ztl_ok, 1)

            def dt_lo(m):
                dve.wait_ge(dth_ok, m + 1)
                TT(r(dt_l[:, :, :]), dt_f[:, :, :], dt_h[:, :, :], ALU.subtract).then_inc(dtl_ok, 1)

            def z_lo(m, a):
                dve.wait_ge(zh_ok[a], m + 1)
                TT(r(z_l[:, a, :, :].rearrange("p s (j g) -> p s j g", j=4)),
                   zs[:, a].rearrange("p j s g -> p s j g"),
                   z_h[:, a, :, :].rearrange("p s (j g) -> p s j g", j=4), ALU.subtract
                   ).then_inc(zl_ok[a], 1)

            def body(i, blocks, supers):
                for k in range(4):
                    n = 4 * i + k
                    if blocks(n - 3):
                        scale_t(n - 3, (k - 3) % 2, 1)
                    if blocks(n - 1):
                        inverse_e(n - 1)
                    if blocks(n - 2):
                        add_bias(n - 2, k % 2, 0)
                        add_bias(n - 2, k % 2, 1)
                    if blocks(n - 2):
                        mixed_lo(n - 2, 1)
                    if k == 0 and supers(i - 3):
                        h1_lo(i - 3, 1)
                    if k == 3 and supers(i - 1):
                        z_lo(i - 1, 1)
                    if k == 1 and supers(i - 1):
                        z_lo(i - 1, 0)
                    if k == 1 and supers(i):
                        stats_x(i)
                    if k == 1 and supers(i - 2):
                        zt_lo(i - 2, 0)
                    if blocks(n - 2):
                        sum_s(n - 2, 0)
                    if blocks(n):
                        times_e(n, k, 0)
                    if blocks(n - 2):
                        scale_t(n - 2, k % 2, 0)
                    if k == 1 and supers(i - 2):
                        zt_lo(i - 2, 1)
                    if k == 0 and supers(i - 2):
                        stats_h(i - 2, 1)
                    if k == 2 and supers(i - 1):
                        stats_h(i - 1, 0)
                    if blocks(n - 2):
                        add_bias(n - 2, k % 2, 2)
                        add_bias(n - 2, k % 2, 3)
                    if blocks(n - 1):
                        mixed_lo(n - 1, 0)
                    if k == 2 and supers(i - 2):
                        h1_lo(i - 2, 0)
                    if k == 1 and supers(i):
                        norm_x(i)
                    if k == 0 and supers(i - 2):
                        norm_h(i - 2, 1)
                    if k == 2 and supers(i - 1):
                        norm_h(i - 1, 0)
                    if blocks(n):
                        times_e(n, k, 1)
                    if blocks(n - 2):
                        sum_s(n - 2, 1)
                    if blocks(n):
                        reduce_e(n)
                    if k == 3 and supers(i - 1):
                        dt_lo(i - 1)
                    if isinstance(i, int):
                        late(n)

            over_supers(dve, body)


def order():
    g, j = np.divmod(np.arange(SUP), 4)
    return (SUP * np.arange(NSUP)[:, None] + P * (g // 32) + 32 * j + g % 32).reshape(-1)


def kernel(**inputs):
    import concourse.bacc as bacc
    from concourse.bass_utils import run_bass_kernel_spmd

    g = {k: np.asarray(v) for k, v in inputs.items()}
    tables = [g[f"tbl_{f}"] for f in range(NS)]
    at = order()
    row = np.arange(BLK * NS).reshape(TILES, P).T
    starts = np.concatenate([[0], np.cumsum([t.shape[0] for t in tables])[:-1]]).astype(np.int32)
    first = np.array([first_sample(t) for t in range(TILES)])
    p, q = np.meshgrid(np.arange(PR), np.arange(PR), indexing="ij")
    hi, lo = np.maximum(p, q) + 1, np.minimum(p, q) + 1
    wl = np.concatenate([g["L0_rec_Wl"], np.zeros((MAXD, 1), np.float32)], axis=1).T
    pair = np.where(p == q, wl.shape[0] - 1, hi * (hi - 1) // 2 + lo)
    wfull = wl[pair].reshape(PR, 4, QS, MAXD).transpose(1, 0, 2, 3).reshape(P, QS, MAXD)
    part, slot = np.meshgrid(np.arange(P), np.arange(SLOTS), indexing="ij")
    low = part < SPLIT
    vec = np.where(low, part // ROW_LO, LOW + (part - SPLIT) // ROW_HI)
    col = np.where(low, SLOTS * (part % ROW_LO), 1 + SLOTS * ((part - SPLIT) % ROW_HI)) + slot
    mixed = (col >= 4) & ~(low & (col >= 4 + LOW))
    other = np.clip(col - 4, 0, PR - 1)
    none = wl.shape[0] - 1
    of_x = np.arange(PR) * (np.arange(PR) + 1) // 2
    wrows = wl[np.where(mixed, pair[vec, other], np.where(col == 2, of_x[vec], none))]
    half = np.where(mixed & ((vec < LOW) == (other < LOW)), 0.5, 1.0).astype(np.float32)
    gq = np.where(mixed, g["L0_rec_gsi"][other], np.float32(1.0))
    wx = np.zeros((P, MAXD), np.float32)
    wx[0:PR] = wl[of_x]
    sel = np.zeros((P, 4, P), np.float32)
    for v in range(PR):
        row_v = ROW_LO * v if v < LOW else SPLIT + ROW_HI * (v - LOW)
        sel[v::PR, 0 if v >= LOW else 1, row_v] = 1.0
        sel[v::PR, 2, 0] = 1.0
        sel[v, 3, 0] = 1.0
    dense_t = g["r_dense_t"].T
    w1 = g["W_top1"]
    w1 = np.concatenate([w1[0:KEEP], w1[MAXD:MAXD + DD]], axis=0)

    def tiles_of(w):
        return w.reshape(w.shape[0] // P, P, w.shape[1]).transpose(1, 0, 2)

    def cols(v, n):
        return v.reshape(n, P).T

    def four(v):
        return np.tile(v, 4)[:, None]

    def by_quadrant(v):
        return np.repeat(v.reshape(4, QS), PR, axis=0)

    vecs = [g["L0_rec_gs"][:, None], g["L0_rec_gd"][:, None], g["L0_rec_bd"][:, None],
            four(g["L0_rec_gsi"]), four(g["L0_rec_bsi"]), g["L0_rec_bs"][:, None],
            cols(g["L0_rec_gl"][0:KEEP], 3), cols(g["L0_rec_bl"][0:KEEP], 3),
            cols(g["b_top1"], 4), cols(g["b_top2"], 2), cols(g["W_top3"][:, 0], 2),
            g["L0_rec_gsi"][vec[:, 0]][:, None]]
    arrays = {
        "tables": np.concatenate(tables, axis=0),
        "ids": g["ids"][at].reshape(NBLK * TILES, P).T,
        "row0": starts[row % NS],
        "eye": np.eye(P, dtype=np.float32),
        "wst": g["L0_rec_Ws"].T,
        "gs": g["L0_rec_gs"],
        "vecs": np.concatenate(vecs, axis=1),
        "wdt": tiles_of(g["L0_rec_Wd"].T),
        "mixrows": g["L0_rec_Wsi"].T[row % NS],
        "mixmask": (row // NS - first[None, :])[:, :, None] == np.arange(6),
        "wsi": g["L0_rec_Wsi"],
        "wfull": wfull,
        "wrows": wrows,
        "half": half,
        "wx": wx,
        "gq": gq,
        "bq": by_quadrant(g["L0_rec_bsi"]),
        "sel": sel,
        "w1": tiles_of(w1),
        "w2": tiles_of(g["W_top2"]),
        "dense": tiles_of(dense_t),
        "dense_pos": tiles_of(dense_t[:, at]),
    }
    arrays["mixmask"] = arrays["mixmask"].astype(np.float32)
    nc = bacc.Bacc("TRN2", target_bir_lowering=False, num_devices=1)
    aps, feed = {}, {}
    for name, a in arrays.items():
        a = np.ascontiguousarray(a)
        feed[f"in_{name}"] = a
        aps[name] = nc.dram_tensor(f"in_{name}", a.shape, mybir.dt.from_np(a.dtype), kind="ExternalInput").ap()
    out = nc.dram_tensor("out_y", (1, B), F32, kind="ExternalOutput").ap()
    dlrm(nc, aps, out)
    res = run_bass_kernel_spmd(nc, [feed], core_ids=[0])
    return res.results[0]["out_y"].reshape(B, 1)
```
